# Optimizing a Trainium2 kernel written in Bass

```python
import numpy as np
import jax
import jax.numpy as jnp

def _softmax(x, axis=-1):
    return jax.nn.softmax(x, axis=axis)
def _gelu(x):
    return jax.nn.gelu(x, approximate=True)
def _silu(x):
    return jax.nn.silu(x)
def _sigmoid(x):
    return jax.nn.sigmoid(x)
def _layernorm(x, axis=-1, eps=1e-5):
    m = jnp.mean(x, axis=axis, keepdims=True)
    v = jnp.var(x, axis=axis, keepdims=True)
    return (x - m) / jnp.sqrt(v + eps)
def _scatter_add(tgt, idx, src, axis=0):
    return tgt.at[idx].add(src)
def _segment_sum(src, seg, n):
    return jax.ops.segment_sum(src, seg, n)

kernel_name = 'mk_conv_seq_d1_conv_nchw512_372756'

def setup_inputs(seed: int = 0):
    np.random.seed(seed)
    _w = jnp.asarray
    def _rec_inputs():
        import jax
        import jax.numpy as jnp
        _gk = jax.random.key(seed)
        x = 7.22e-05 + 1 * jax.random.normal(jax.random.fold_in(_gk, 1), (16, 512, 32, 32), jnp.float32)
        return x
    x = _rec_inputs()
    def _L0_conv_setup():
        import jax, jax.numpy as jnp
        import numpy as np
        NUM_GROUPS = 32
        EPS = 1e-06
        NUM_HEADS = 8

        def group_norm32(x, gamma, beta):
            b, c, h, w = x.shape
            xf = x.astype(jnp.float32).reshape(b, NUM_GROUPS, -1)
            mean = xf.mean(axis=-1, keepdims=True)
            var = xf.var(axis=-1, keepdims=True)
            xn = ((xf - mean) * jax.lax.rsqrt(var + EPS)).reshape(b, c, h, w)
            xn = xn * gamma[None, :, None, None] + beta[None, :, None, None]
            return xn.astype(x.dtype)
        key = jax.random.key(seed)
        ks = jax.random.split(key, 4)
        b, c, h, w = (16, 512, 32, 32)
        x = jax.random.normal(ks[0], (b, c, h, w), dtype=jnp.float32)
        w_qkv = jax.random.normal(ks[1], (3 * c, c), dtype=jnp.float32) * (1.0 / np.sqrt(c))
        b_qkv = jnp.zeros((3 * c,), dtype=jnp.float32)
        w_proj = jax.random.normal(ks[2], (c, c), dtype=jnp.float32) * (1.0 / np.sqrt(c))
        b_proj = jnp.zeros((c,), dtype=jnp.float32)
        gamma = jnp.ones((c,), dtype=jnp.float32)
        beta = jnp.zeros((c,), dtype=jnp.float32)
        return {'x': x, 'w_qkv': w_qkv, 'b_qkv': b_qkv, 'w_proj': w_proj, 'b_proj': b_proj, 'gamma': gamma, 'beta': beta}
    _L0_conv_all = _L0_conv_setup()
    _L0_conv_in = {k: v for k, v in _L0_conv_all.items() if k in ('w_qkv', 'b_qkv', 'w_proj', 'b_proj', 'gamma', 'beta', )}
    del _L0_conv_all

    return {
        "x": x,
        "L0_conv_w_qkv": _L0_conv_in["w_qkv"],
        "L0_conv_b_qkv": _L0_conv_in["b_qkv"],
        "L0_conv_w_proj": _L0_conv_in["w_proj"],
        "L0_conv_b_proj": _L0_conv_in["b_proj"],
        "L0_conv_gamma": _L0_conv_in["gamma"],
        "L0_conv_beta": _L0_conv_in["beta"],
    }

def reference(x, L0_conv_w_qkv, L0_conv_b_qkv, L0_conv_w_proj, L0_conv_b_proj, L0_conv_gamma, L0_conv_beta):
    import jax
    import jax.numpy as jnp
    def _L0_conv_ref(x, w_qkv, b_qkv, w_proj, b_proj, gamma, beta):
        import jax, jax.numpy as jnp
        import numpy as np
        NUM_GROUPS = 32
        EPS = 1e-06
        NUM_HEADS = 8

        def group_norm32(x, gamma, beta):
            b, c, h, w = x.shape
            xf = x.astype(jnp.float32).reshape(b, NUM_GROUPS, -1)
            mean = xf.mean(axis=-1, keepdims=True)
            var = xf.var(axis=-1, keepdims=True)
            xn = ((xf - mean) * jax.lax.rsqrt(var + EPS)).reshape(b, c, h, w)
            xn = xn * gamma[None, :, None, None] + beta[None, :, None, None]
            return xn.astype(x.dtype)
        b, c, h, w = x.shape
        H = NUM_HEADS
        d = c // H
        n = h * w
        x_norm = group_norm32(x, gamma, beta)
        qkv = jnp.einsum('oc,bchw->bohw', w_qkv, x_norm) + b_qkv[None, :, None, None]
        q, k, v = jnp.split(qkv, 3, axis=1)
        q = q.reshape(b, H, d, n)
        k = k.reshape(b, H, d, n)
        v = v.reshape(b, H, d, n)
        scale = d ** (-0.5)
        attn = jnp.einsum('bhdn,bhdm->bhnm', q, k) * scale
        attn = jax.nn.softmax(attn, axis=-1)
        out = jnp.einsum('bhnm,bhdm->bhdn', attn, v).reshape(b, c, h, w)
        proj = jnp.einsum('oc,bchw->bohw', w_proj, out) + b_proj[None, :, None, None]
        return x + proj

    def _gn(v, G=32, eps=1e-5):
        B_, C_, H_, W_ = v.shape
        g = v.reshape(B_, G, C_ // G, H_, W_)
        m = jnp.mean(g, axis=(2, 3, 4), keepdims=True)
        s = jnp.var(g, axis=(2, 3, 4), keepdims=True)
        return ((g - m) / jnp.sqrt(s + eps)).reshape(v.shape)

    def _ln_c(v, eps=1e-6):
        m = jnp.mean(v, axis=1, keepdims=True)
        s = jnp.var(v, axis=1, keepdims=True)
        return (v - m) / jnp.sqrt(s + eps)

    def _ln_t(v, eps=1e-5):
        m = jnp.mean(v, axis=-1, keepdims=True)
        s = jnp.var(v, axis=-1, keepdims=True)
        return (v - m) / jnp.sqrt(s + eps)

    def _to_tokens(v):
        B_, C_, H_, W_ = v.shape
        return v.reshape(B_, C_, H_ * W_).transpose(0, 2, 1)
    def _from_tokens(t, like):
        B_, C_, H_, W_ = like.shape
        return t.transpose(0, 2, 1).reshape(B_, C_, H_, W_)

    x = _L0_conv_ref(x, L0_conv_w_qkv, L0_conv_b_qkv, L0_conv_w_proj, L0_conv_b_proj, L0_conv_gamma, L0_conv_beta)
    return x


_drawn_inputs = setup_inputs


def setup_inputs(seed=0):
    import zlib

    import numpy as np

    out = dict(_drawn_inputs(seed))
    spreads = {'L0_conv_b_qkv': (0.0, 0.1),
     'L0_conv_b_proj': (0.0, 0.1),
     'L0_conv_gamma': (1.0, 0.2),
     'L0_conv_beta': (0.0, 0.1)}
    factors = {}
    for name, (base, spread) in spreads.items():
        noise = np.random.default_rng([zlib.crc32(name.encode()), seed]).standard_normal(out[name].shape)
        drawn = base * np.exp(spread * noise) if base else spread * noise
        out[name] = jnp.asarray(drawn.astype(out[name].dtype))
    for name, factor in factors.items():
        out[name] = (out[name] * factor).astype(out[name].dtype)
    return out
```

```python
import math
from contextlib import ExitStack

import concourse.bass as bass
from concourse import mybir

F32 = mybir.dt.float32
F32R = mybir.dt.float32r
F16 = mybir.dt.float16
BF16 = mybir.dt.bfloat16
ALU = mybir.AluOpType
ACT = mybir.ActivationFunctionType
AX = mybir.AxisListType

P = 128
BANK = 512
HEADS = 8
GROUPS = 32
EPS = 1e-6

W_UNIT = 256.0
X_UNIT = 32.0
V_UNIT = 1.0 / 256.0
P_UNIT = 16.0


def groupnorm_attention(
    nc: bass.Bass,
    x: bass.AP,
    w_qkv: bass.AP,
    b_qkv: bass.AP,
    w_proj: bass.AP,
    b_proj: bass.AP,
    gamma: bass.AP,
    beta: bass.AP,
    out: bass.AP,
):
    BATCH, C, HI, WI = x.shape
    N = HI * WI
    D = C // HEADS
    CT = C // P
    NT = N // P
    HALVES = N // BANK
    GSIZE = C // GROUPS
    PAIRS = HEADS // 2
    HSTEPS = HALVES * NT
    PSTEPS = 2 * HSTEPS
    STEPS = HEADS * HSTEPS
    WT = 4 * CT
    assert D * 2 == P and CT == PAIRS == 4 and HALVES == 2 and NT == 8

    x_d = x.rearrange("b (t p) h w -> b t p (h w)", p=P)
    out_d = out.rearrange("b (t p) h w -> b t p (h w)", p=P)
    wqkv_d = w_qkv.rearrange("(t p) c -> t p c", p=P)
    wproj_d = w_proj.rearrange("(t p) c -> t p c", p=P)

    with ExitStack() as ctx:

        def sb(name, shape, dt):
            return ctx.enter_context(nc.sbuf_tensor(name, shape, dt))

        def sem(name):
            return ctx.enter_context(nc.semaphore(name))

        xin = sb("xin", [P, CT, N], F32)
        xres = sb("xres", [P, CT, N], F32)
        xs = sb("xs", [P, 2, N], F32)
        xh = sb("xh", [P, 2, CT, N], F16)
        wT = sb("wT", [P, 2, CT, WT * P], F16)
        K1, K2, Q1, Q2 = range(4)
        qk = sb("qk", [P, 2, 2, 4, N], F32R)
        qk32 = sb("qk32", [P, 2, BANK], F32)
        VW = 2 * D + 1
        vb = sb("vb", [P, 2, NT, 2, VW], F16)
        RING = 4
        p32 = sb("p32", [P, RING, BANK], F32)
        phi = sb("phi", [P, RING, BANK], F16)
        plo = sb("plo", [P, RING, BANK], F16)
        on = sb("on", [P, 2, NT, P], F32)
        oT = sb("oT", [P, 2, CT, N], F16)
        yb = xs
        mx2 = sb("mx2", [P, NT, 2], F32)
        nmx = sb("nmx", [P, NT], F32)
        mxp = sb("mxp", [P, 2 * NT], BF16)
        rec = sb("rec", [P, 4], F32)
        bnst = sb("bnst", [P, CT, 2, 6], F32)
        mv = sb("mv", [P, CT, 2], F32)
        gn = sb("gn", [P, 10, CT], F32)
        GMEAN, DEV, SQ, VARC, VAR, RS0, RS1, RS2, RS3, RSTD = range(10)
        n2 = sb("n2", [P, WT], F32)
        bsum = sb("bsum", [P, WT], F32)
        bias = sb("bias", [P, WT], F32)
        bload = sb("bload", [P, WT], F32)
        fsc = sb("fsc", [P, WT], F32)
        rsc = sb("rsc", [P, WT], F32)
        osc = sb("osc", [P, WT], F32)
        vsc = sb("vsc", [P, CT], F32)
        ident32 = sb("ident32", [P, P], F32)
        ident16 = sb("ident16", [P, P], F16)
        identb = sb("identb", [P, P], BF16)
        ones32 = sb("ones32", [P, P], F32)
        gmat = sb("gmat", [P, P], F32)
        mask = sb("mask", [P, NT], F32)
        carrier = sb("carrier", [P, 1], F32)
        halfs = sb("halfs", [P, CT], F32)
        w_nat = xres[:, :, C:2 * C]
        gamma_r, beta_r, vnorm_r, vbias_r = (xres[:, i, 0:C] for i in range(4))
        w_scaled = xs[:, :, C:2 * C]
        diag = on[:, 0, :, :]

        def bank(name):
            return ctx.enter_context(nc.psum_tensor(name, [P, BANK], F32))

        S = [bank("S0"), bank("S1")]
        M = [bank("M0"), bank("M1")]
        O = [bank("O0"), bank("O1")]
        G = [bank("G0"), bank("G1")]

        scrap, scrap2 = O[0][:, 0:C], O[1][:, 0:C]

        s_const = sem("s_const")
        s_made = sem("s_made")
        s_row = sem("s_row")
        s_w = [sem(f"s_w{i}") for i in range(4)]
        s_wg, s_n2, s_f, s_wsc, s_whi, s_wlo, s_wtr, s_wtev_hi, s_wtev_lo = (
            sem(n) for n in ("s_wg", "s_n2", "s_f", "s_wsc", "s_whi", "s_wlo", "s_wtr", "s_wtev_hi", "s_wtev_lo"))
        s_fold = sem("s_fold")
        s_diag, s_rows, s_rowcp = sem("s_diag"), sem("s_rows"), sem("s_rowcp")
        x_loaded = [sem(f"x_loaded{i}") for i in range(CT)]
        res_copied = sem("res_copied")
        bn_done, stats_done, mean_mm, dev_done, var_mm, var_read = (
            sem(n) for n in ("bn_done", "stats_done", "mean_mm", "dev_done", "var_mm", "var_read"))
        gn_link, powered, s_pow = sem("gn_link"), sem("powered"), sem("s_pow")
        xs_done, xhi_done, xh_ready = sem("xs_done"), sem("xhi_done"), sem("xh_ready")
        qk_mm, qk_evac, k_hi, qk_split, q_lo = (
            sem(n) for n in ("qk_mm", "qk_evac", "k_hi", "qk_split", "q_lo"))
        v_mm, v_hi, v_ready = sem("v_mm"), sem("v_hi"), sem("v_ready")
        max_mm, reduced, mx_neg, mx_hi, mx_cast, mx_tr, mx_ready = (
            sem(n) for n in ("max_mm", "reduced", "mx_neg", "mx_hi", "mx_cast", "mx_tr", "mx_ready"))
        scores_mm, exp_done, plo_done, pv_mm = (
            sem(n) for n in ("scores_mm", "exp_done", "plo_done", "pv_mm"))
        o_rec, o_evac = sem("o_rec"), sem("o_evac")
        ot_mm, ot_hi, ot_ready = sem("ot_mm"), sem("ot_hi"), sem("ot_ready")
        y_mm, y_evac = sem("y_mm"), sem("y_evac")
        y_stored = [sem("y_stored0"), sem("y_stored1")]

        TILE_ORDER = [*range(2 * CT, 3 * CT), *range(2 * CT), *range(3 * CT, 4 * CT)]

        def counts(eng, b):
            kept = {}

            def at(k, c):
                if isinstance(b, int):
                    return k * b + c
                if k not in kept:
                    kept[k] = eng.snap(b * k)
                return kept[k] + c
            return at

        def wait(eng, semaphore, count):
            if isinstance(count, int) and count <= 0:
                return
            eng.wait_ge(semaphore, count)

        QK_STEPS = 3
        OT_AT = 4 * QK_STEPS
        V_AT = OT_AT + HALVES
        Y_AT = V_AT + NT
        MX_TR_AT = NT + 1

        block = ctx.enter_context(nc.Block())

        @block.sync
        def _(sp):
            sp.dma_start(gamma_r, gamma.rearrange("(a c) -> a c", a=1).broadcast_to([P, C])).then_inc(s_row, 16)
            sp.dma_start(beta_r, beta.rearrange("(a c) -> a c", a=1).broadcast_to([P, C])).then_inc(s_row, 16)
            sp.dma_start(bload[:, 0:3 * CT], b_qkv.rearrange("(t p) -> p t", p=P),
                         allow_slow_non_contiguous=True).then_inc(s_row, 16)
            sp.dma_start(bload[:, 3 * CT:WT], b_proj.rearrange("(t p) -> p t", p=P),
                         allow_slow_non_contiguous=True).then_inc(s_row, 16)

            def load_w(i):
                t = TILE_ORDER[i]
                if i >= 4:
                    sp.wait_ge(s_wg, 2 * (i - 4) + 2)
                src = wqkv_d[t] if t < 3 * CT else wproj_d[t - 3 * CT]
                sp.dma_start(w_nat[:, i % 4, :], src).then_inc(s_w[i % 4], 16)

            for i in range(4):
                load_w(i)
            for t in range(CT):
                sp.dma_start(xin[:, t, :], x_d[0, t]).then_inc(x_loaded[t], 16)
            for i in range(4, WT):
                load_w(i)

            def store(at, last_b):
                for t in range(CT):
                    wait(sp, y_evac, at(2 * CT, -2 * CT + 2 * t + 2))
                    sp.dma_start(out_d[last_b, t], yb[:, t % 2, :]).then_inc(y_stored[t % 2], 16)

            def batch(b, first=False, last=False):
                at = counts(sp, b)
                if not first:
                    store(at, b - 1)
                if not last:
                    for t in range(CT):
                        wait(sp, res_copied, at(CT, t + 1))
                        sp.dma_start(xin[:, t, :], x_d[b + 1, t]).then_inc(x_loaded[t], 16)

            batch(0, first=True)
            with sp.Fori(1, BATCH - 1) as b:
                batch(b)
            batch(BATCH - 1, last=True)
            store(counts(sp, BATCH), BATCH - 1)
            for i in range(2):
                sp.wait_ge(y_stored[i], 16 * BATCH * CT // 2)

        @block.tensor
        def _(pe):
            def mean_matmul(at, n):
                wait(pe, stats_done, at(1, n + 1))
                nc.tensor.matmul(M[1][:, 0:CT], gmat[:, :], mv[:, :, 0], start=True, stop=True).then_inc(mean_mm, 1)

            def var_matmul(at, n):
                wait(pe, dev_done, at(1, n + 1))
                nc.tensor.matmul(M[1][:, 0:CT], gmat[:, :], gn[:, VARC, :], start=True, stop=True).then_inc(var_mm, 1)

            def project_qk(at, pair, group, part, parts=QK_STEPS):
                col = (pair % PAIRS + PAIRS * (group // 2)) * P
                half = group % 2
                todo = [(k, w, h) for k in range(CT) for w, h in ((0, 0), (0, 1), (1, 0))]
                n = len(todo) // parts
                for i in range(part * n, part * n + n):
                    k, w, h = todo[i]
                    mm = nc.tensor.matmul(G[half][:, :], wT[:, w, k, col:col + P],
                                          xh[:, h, k, half * BANK:(half + 1) * BANK],
                                          start=(i == 0), stop=(i == len(todo) - 1))
                if part == parts - 1:
                    mm.then_inc(qk_mm, 1)

            def project_v(at, pair, mt):
                col = (2 * PAIRS + pair % PAIRS) * P
                dst = G[mt // 4][:, (mt % 4) * P:(mt % 4 + 1) * P]
                todo = [(k, w, h) for k in range(CT) for h, w in ((0, 0), (0, 1), (1, 0))]
                for i, (k, w, h) in enumerate(todo):
                    mm = nc.tensor.matmul(dst, xh[:, h, k, mt * P:(mt + 1) * P], wT[:, w, k, col:col + P],
                                          start=(i == 0), stop=(i == len(todo) - 1))
                if mt % 4 == 3:
                    mm.then_inc(v_mm, 1)

            def max_tiles(at, head, t):
                par, hd = head // 2 % 2, head % 2
                for half in range(HALVES):
                    wait(pe, reduced, at(STEPS, HSTEPS * head + 2 * t + half - 1))
                    nc.tensor.matmul(M[half][:, :], qk[:, par, hd, Q1, t * P:(t + 1) * P],
                                     qk[:, par, hd, K1, half * BANK:(half + 1) * BANK],
                                     start=True, stop=True).then_inc(max_mm, 1)

            def max_transpose(at, head):
                row = 0 if head % 2 else D
                wait(pe, mx_cast, at(HEADS, head + 1))
                dst = M[0][row:row + 2 * NT, 0:P // 2].bitcast(BF16)
                nc.tensor.transpose(dst, mxp[:, :], identb[:, :]).then_inc(mx_tr, 1)

            def scores(at, s):
                head, u = s // HSTEPS, s % HSTEPS
                par, hd, half, mt = head // 2 % 2, head % 2, u // NT, u % NT
                wait(pe, exp_done, at(STEPS, s - 1))
                if u == 0:
                    wait(pe, mx_ready, at(HEADS, head + 1))
                q, k = slice(half * BANK, (half + 1) * BANK), slice(mt * P, (mt + 1) * P)
                nc.tensor.matmul(S[s % 2][:, :], qk[:, par, hd, K1, k], qk[:, par, hd, Q1, q], start=True, stop=False)
                nc.tensor.matmul(S[s % 2][:, :], qk[:, par, hd, K2, k], qk[:, par, hd, Q2, q],
                                 start=False, stop=True).then_inc(scores_mm, 1)

            def values(at, s):
                head, u = s // HSTEPS, s % HSTEPS
                par, hd, half, mt = head // 2 % 2, head % 2, u // NT, u % NT
                if mt == 0:
                    wait(pe, o_evac, at(2 * HEADS, 2 * head + half - 1))
                wait(pe, plo_done, at(STEPS, s + 1))
                for j in range(4):
                    cols = slice(j * P, (j + 1) * P)
                    o = O[half][:, j * (D + 1):(j + 1) * (D + 1)]
                    hi = phi[:, s % RING, cols]
                    nc.tensor.matmul(o, hi, vb[:, par, mt, hd, 0:D + 1],
                                     start=(mt == 0 and j == 0), stop=False, skip_group_check=True)
                    nc.tensor.matmul(o[:, 0:D], hi, vb[:, par, mt, hd, D + 1:VW],
                                     start=False, stop=False, skip_group_check=True)
                    mm = nc.tensor.matmul(o, plo[:, s % RING, cols], vb[:, par, mt, hd, 0:D + 1],
                                          start=False, stop=(mt == NT - 1), skip_group_check=True)
                mm.then_inc(pv_mm, 1)

            def transpose_outputs(at, pair, half):
                wait(pe, o_evac, at(2 * HEADS, 4 * pair + 4))
                for j in range(4):
                    mm = nc.tensor.transpose(G[half][:, j * P:(j + 1) * P], on[:, pair % 2, 4 * half + j, :],
                                             ident32[:, :])
                mm.then_inc(ot_mm, 1)

            def project_out(i):
                t, half = i // 2, i % 2
                col = (3 * CT + t) * P
                todo = [(k, w, h) for k in range(CT) for w, h in ((0, 0), (0, 1), (1, 0))]
                for j, (k, w, h) in enumerate(todo):
                    mm = nc.tensor.matmul(G[half][:, :], wT[:, w, k, col:col + P],
                                          oT[:, h, k, half * BANK:(half + 1) * BANK],
                                          start=(j == 0), stop=(j == len(todo) - 1))
                mm.then_inc(y_mm, 1)

            pe.wait_ge(s_const, 1)
            for i in range(WT):
                if i == CT:
                    pe.wait_ge(s_diag, 1)
                    for j in range(2 * CT):
                        mm = nc.tensor.matmul(M[j // CT][:, (j % CT) * P:(j % CT + 1) * P], ones32[:, :],
                                              diag[:, j, :], start=True, stop=True)
                    mm.then_inc(s_rows, 1)
                pe.wait_ge(s_wlo, i + 1)
                if i >= 2:
                    pe.wait_ge(s_wtev_hi, i - 1)
                    pe.wait_ge(s_wtev_lo, i - 1)
                for dst, src in ((S[i % 2], phi), (G[i % 2], plo)):
                    for k in range(CT):
                        mm = nc.tensor.transpose(dst[:, 0:C // 2].bitcast(F16)[:, k * P:(k + 1) * P], src[:, i % RING, k * P:(k + 1) * P],
                                                 ident16[:, :])
                mm.then_inc(s_wtr, 1)
            at = counts(pe, 0)
            mean_matmul(at, 0)
            var_matmul(at, 0)
            pe.wait_ge(s_wtev_hi, WT)
            pe.wait_ge(s_wtev_lo, WT)
            pe.wait_ge(xh_ready, CT)
            for group in range(4):
                wait(pe, qk_evac, group - 1)
                project_qk(at, 0, group, 0, parts=1)
            for mt in range(NT):
                if mt % 4 == 0:
                    pe.wait_ge(qk_evac, 3 + mt // 4)
                project_v(at, 0, mt)
            pe.wait_ge(qk_split, 4)
            pe.wait_ge(q_lo, 2)
            pe.wait_ge(var_read, 1)
            for t in range(NT):
                max_tiles(at, 0, t)
            max_transpose(at, 0)
            scores(at, 0)
            scores(at, 1)

            def batch(b, first=False, last=False):
                at = counts(pe, b)
                for p in range(PAIRS):
                    has_next = not (last and p == PAIRS - 1)
                    has_prev = not (first and p == 0)
                    for t in range(PSTEPS):
                        s = PSTEPS * p + t
                        head, u = s // HSTEPS, s % HSTEPS
                        more = has_next or head < HEADS - 1
                        if s + 2 < STEPS or not last:
                            scores(at, s + 2)
                        if t == 0:
                            wait(pe, v_ready, at(2 * PAIRS, 2 * p + 2))
                        if u == 0 and more:
                            if (head + 1) % 2 == 0:
                                wait(pe, qk_split, at(4 * PAIRS, 4 * (p + 1) + 4))
                                wait(pe, q_lo, at(2 * PAIRS, 2 * (p + 1) + 2))
                            if p == 2 and t == HSTEPS and not last:
                                wait(pe, var_read, at(1, 2))
                        if u < NT and more:
                            max_tiles(at, head + 1, u)
                        if u == MX_TR_AT and more:
                            max_transpose(at, head + 1)
                        if t < OT_AT and has_next:
                            group, part = t // QK_STEPS, t % QK_STEPS
                            if part == 0:
                                if group >= 2:
                                    wait(pe, qk_evac, at(4 * PAIRS, 4 * (p + 1) + group - 1))
                                elif p == 1 and not first:
                                    wait(pe, y_evac, at(2 * CT, -1 + group))
                                else:
                                    wait(pe, v_ready, at(2 * PAIRS, 2 * p + group + 1))
                                if group == 0 and p == PAIRS - 1:
                                    wait(pe, xh_ready, at(CT, 2 * CT))
                            project_qk(at, p + 1, group, part)
                        if OT_AT <= t < V_AT and has_prev:
                            half = t - OT_AT
                            if has_next:
                                wait(pe, qk_evac, at(4 * PAIRS, 4 * (p + 1) + 3 + half))
                            else:
                                wait(pe, v_ready, at(2 * PAIRS, 2 * p + half + 1))
                            transpose_outputs(at, p - 1, half)
                        if V_AT <= t < Y_AT and has_next:
                            mt = t - V_AT
                            if mt % 4 == 0:
                                if has_prev:
                                    wait(pe, ot_ready, at(2 * PAIRS, 2 * (p - 1) + mt // 4 + 1))
                                else:
                                    wait(pe, qk_evac, at(4 * PAIRS, 4 * (p + 1) + 3 + mt // 4))
                            project_v(at, p + 1, mt)
                        if Y_AT <= t < Y_AT + 2 * CT and p == 0 and not first:
                            i = t - Y_AT
                            if i < 2:
                                wait(pe, v_ready, at(2 * PAIRS, 2 + i + 1))
                            else:
                                wait(pe, y_evac, at(2 * CT, -2 * CT + i - 1))
                            if i < 2:
                                wait(pe, ot_ready, at(2 * PAIRS, 0))
                            project_out(i)
                        if p == 2 and t == NT + 2 and not last:
                            wait(pe, reduced, at(STEPS, HSTEPS * (head + 1) + HSTEPS))
                            mean_matmul(at, 1)
                        if p == 2 and t == NT + 5 and not last:
                            var_matmul(at, 1)
                        values(at, s)

            batch(0, first=True)
            with pe.Fori(1, BATCH - 1) as b:
                batch(b)
            batch(BATCH - 1, last=True)
            at = counts(pe, BATCH)
            for half in range(HALVES):
                pe.wait_ge(ot_ready, 2 * PAIRS * BATCH - 4 + half + 1)
                transpose_outputs(at, -1, half)
            for i in range(2 * CT):
                if i < 2:
                    pe.wait_ge(ot_ready, 2 * PAIRS * BATCH)
                else:
                    pe.wait_ge(y_evac, 2 * CT * (BATCH - 1) + i - 1)
                project_out(i)

        @block.scalar
        def _(act):
            def evac_qk(at, pair, group):
                t = pair % PAIRS + PAIRS * (group // 2)
                n = 4 * pair + group
                wait(act, qk_mm, at(4 * PAIRS, n + 1))
                wait(act, qk_split, at(4 * PAIRS, n - 1))
                wait(act, q_lo, at(2 * PAIRS, 2 * pair + max(0, group - 1)))
                nc.scalar.activation(qk32[:, group % 2, :], G[group % 2][:, :], ACT.Identity,
                                     bias=bias[:, t:t + 1], scale=osc[:, t:t + 1]).then_inc(qk_evac, 1)

            def evac_v(at, pair, i):
                wait(act, v_mm, at(2 * PAIRS, 2 * pair + i + 1))
                wait(act, pv_mm, at(STEPS, PSTEPS * (pair - 1)))
                dst = vb[:, pair % 2, 4 * i:4 * i + 4, :, 0:D]
                src = G[i][:, :].rearrange("p (m h d) -> p m h d", m=4, h=2)
                nc.scalar.mul(dst, src, V_UNIT).then_inc(v_hi, 1)

            def evac_ot(at, pair, half):
                wait(act, ot_mm, at(2 * PAIRS, 2 * pair + half + 1))
                if pair == 0:
                    wait(act, y_mm, at(2 * CT, 0))
                nc.scalar.copy(oT[:, 0, pair % PAIRS, half * BANK:(half + 1) * BANK], G[half][:, :]).then_inc(ot_hi, 1)

            for i in range(WT):
                t = TILE_ORDER[i]
                act.wait_ge(s_wg, 2 * i + 1)
                if i >= 1:
                    act.wait_ge(s_n2, i)
                nc.scalar.activation(scrap2, xs[:, i % 2, 0:C], ACT.Square, accum_out=n2[:, t:t + 1]).then_inc(s_n2, 1)
                act.wait_ge(s_f, i + 1)
                if i >= 2:
                    act.wait_ge(s_wlo, i - 1)
                nc.scalar.activation(w_scaled[:, i % 2, :], xs[:, i % 2, 0:C], ACT.Copy,
                                     scale=fsc[:, t:t + 1]).then_inc(s_wsc, 1)
                act.wait_ge(s_wsc, i + 1)
                if i >= RING:
                    act.wait_ge(s_wtr, i - RING + 1)
                nc.scalar.copy(phi[:, i % RING, :], w_scaled[:, i % 2, :]).then_inc(s_whi, 1)
                act.wait_ge(s_wtr, i + 1)
                src = S[i % 2][:, 0:C // 2].bitcast(F16).rearrange("p (k n) -> p k n", k=CT)
                nc.scalar.copy(wT[:, 0, :, t * P:(t + 1) * P], src).then_inc(s_wtev_hi, 1)
            at = counts(act, 0)
            for group in range(4):
                evac_qk(at, 0, group)
            evac_v(at, 0, 0)
            evac_v(at, 0, 1)

            def batch(b, first=False, last=False):
                at = counts(act, b)
                for p in range(PAIRS):
                    has_next = not (last and p == PAIRS - 1)
                    has_prev = not (first and p == 0)
                    for t in range(PSTEPS):
                        s = PSTEPS * p + t
                        wait(act, scores_mm, at(STEPS, s + 1))
                        wait(act, pv_mm, at(STEPS, s + 1 - RING))
                        for dst in (phi, p32):
                            e = nc.scalar.activation(dst[:, s % RING, :], S[s % 2][:, :], ACT.Exp,
                                                     bias=math.log(P_UNIT), scale=float(D) ** -0.5)
                        e.then_inc(exp_done, 1)
                        f = t - 2
                        if 0 <= f < OT_AT and f % QK_STEPS == QK_STEPS - 1 and has_next:
                            evac_qk(at, p + 1, f // QK_STEPS)
                        if OT_AT <= f < V_AT and has_prev:
                            evac_ot(at, p - 1, f - OT_AT)
                        if f in (V_AT + 3, V_AT + 7) and has_next:
                            evac_v(at, p + 1, (f - V_AT) // 4)

            batch(0, first=True)
            with act.Fori(1, BATCH - 1) as b:
                batch(b)
            batch(BATCH - 1, last=True)
            at = counts(act, BATCH)
            evac_ot(at, -1, 0)
            evac_ot(at, -1, 1)

        @block.vector
        def _(dve):
            fold = [0]

            def link(ins):
                fold[0] += 1
                ins.then_inc(s_fold, 1)
                dve.wait_ge(s_fold, fold[0])

            LINKS = 8

            def group_stats(at, n):
                for t in range(CT):
                    wait(dve, x_loaded[t], at(16, 16 * n + 16))
                    for half in range(2):
                        last = nc.vector.bn_stats(bnst[:, t, half, :], xin[:, t, half * BANK:(half + 1) * BANK])
                last.then_inc(bn_done, 1)
                wait(dve, bn_done, at(1, n + 1))
                nc.vector.memset(carrier[:, :], 0.0)
                for t in range(CT):
                    last = nc.vector.bn_aggr(mv[:, t, :], bnst[:, t, :, :].rearrange("p a b -> p (a b)"))
                last.then_inc(stats_done, 1)

            def gn_wait(at, n, i):
                wait(dve, gn_link, at(LINKS, LINKS * n + i))

            def group_deviation(at, n):
                wait(dve, mean_mm, at(1, n + 1))
                nc.vector.tensor_copy(gn[:, GMEAN, :], M[1][:, 0:CT]).then_inc(gn_link, 1)
                gn_wait(at, n, 1)
                nc.vector.tensor_tensor(gn[:, DEV, :], mv[:, :, 0], gn[:, GMEAN, :], ALU.subtract).then_inc(gn_link, 1)
                gn_wait(at, n, 2)
                nc.vector.tensor_tensor(gn[:, SQ, :], gn[:, DEV, :], gn[:, DEV, :], ALU.mult).then_inc(gn_link, 1)
                gn_wait(at, n, 3)
                nc.vector.tensor_tensor(gn[:, VARC, :], gn[:, SQ, :], mv[:, :, 1], ALU.add).then_inc(dev_done, 1)

            def group_rstd(at, n):
                wait(dve, var_mm, at(1, n + 1))
                nc.vector.tensor_scalar(gn[:, VAR, :], M[1][:, 0:CT], EPS, None, ALU.add).then_inc(var_read, 1)
                wait(dve, var_read, at(1, n + 1))
                wait(dve, powered, at(1, n + 1))
                nc.vector.tensor_tensor(gn[:, RS1, :], gn[:, RS0, :], gn[:, RS0, :], ALU.mult).then_inc(gn_link, 1)
                gn_wait(at, n, 4)
                nc.vector.tensor_tensor(gn[:, RS2, :], gn[:, RS1, :], gn[:, VAR, :], ALU.mult).then_inc(gn_link, 1)
                gn_wait(at, n, 5)
                nc.vector.tensor_scalar(gn[:, RS3, :], gn[:, RS2, :], -0.5 * X_UNIT, 1.5 * X_UNIT,
                                        ALU.mult, ALU.add).then_inc(gn_link, 1)
                gn_wait(at, n, 6)
                nc.vector.tensor_tensor(gn[:, RSTD, :], gn[:, RS0, :], gn[:, RS3, :], ALU.mult).then_inc(gn_link, 1)
                gn_wait(at, n, 7)
                nc.vector.tensor_copy(gn[:, SQ, :], gn[:, RSTD, :]).then_inc(gn_link, 1)
                gn_wait(at, n, 8)

            def normalise(at, n, t):
                if t < 2:
                    wait(dve, y_stored[t], at(32, 32 * (n - 1)))
                wait(dve, xh_ready, at(CT, CT * n + t - 1))
                nc.vector.tensor_scalar(xs[:, t % 2, :], xin[:, t, :], gn[:, GMEAN, t:t + 1], gn[:, RSTD, t:t + 1],
                                        ALU.subtract, ALU.mult).then_inc(xs_done, 1)
                wait(dve, xs_done, at(CT, CT * n + t + 1))
                nc.vector.tensor_copy(xh[:, 0, t, :], xs[:, t % 2, :]).then_inc(xhi_done, 1)
                wait(dve, xhi_done, at(CT, CT * n + t + 1))
                nc.vector.tensor_tensor(xh[:, 1, t, :], xs[:, t % 2, :], xh[:, 0, t, :], ALU.subtract).then_inc(xh_ready, 1)

            def split_qk(at, pair, group):
                par, half = pair % 2, group % 2
                cols = slice(half * BANK, (half + 1) * BANK)
                n = 4 * pair + group
                wait(dve, qk_evac, at(4 * PAIRS, n + 1))
                wait(dve, scores_mm, at(STEPS, PSTEPS * (pair - 1)))
                a, b = qk32[0:D, half, :], qk32[D:P, half, :]
                if group < 2:
                    nc.vector.tensor_copy(qk[0:D, par, 0, Q1, cols], a)
                    nc.vector.tensor_copy(qk[D:P, par, 0, Q1, cols], a)
                    nc.vector.tensor_copy(qk[0:D, par, 1, Q1, cols], b)
                    nc.vector.tensor_copy(qk[D:P, par, 1, Q1, cols], b).then_inc(qk_split, 1)
                else:
                    nc.vector.tensor_copy(qk[0:D, par, 0, K1, cols], a)
                    nc.vector.tensor_copy(qk[0:D, par, 0, K2, cols], a)
                    nc.vector.tensor_copy(qk[D:P, par, 1, K1, cols], b)
                    nc.vector.tensor_copy(qk[D:P, par, 1, K2, cols], b).then_inc(k_hi, 1)
                    wait(dve, k_hi, at(2 * PAIRS, 2 * pair + half + 1))
                    nc.vector.tensor_tensor(qk[D:P, par, 0, K1, cols], a, qk[0:D, par, 0, K1, cols].bitcast(F32),
                                            ALU.subtract)
                    nc.vector.tensor_tensor(qk[0:D, par, 1, K1, cols], b, qk[D:P, par, 1, K1, cols].bitcast(F32),
                                            ALU.subtract).then_inc(qk_split, 1)

            def split_v(at, pair, i):
                wait(dve, v_hi, at(2 * PAIRS, 2 * pair + i + 1))
                v = vb[:, pair % 2, 4 * i:4 * i + 4, :, :].rearrange("p m h c -> p (m h) c")
                src = G[i][:, :].rearrange("p (m d) -> p m d", d=D)
                nc.vector.scalar_tensor_tensor(out=v[:, :, D + 1:VW], in0=src, scalar=V_UNIT, in1=v[:, :, 0:D],
                                               op0=ALU.mult, op1=ALU.subtract).then_inc(v_ready, 1)

            def split_ot(at, pair, half):
                cols = slice(half * BANK, (half + 1) * BANK)
                wait(dve, ot_hi, at(2 * PAIRS, 2 * pair + half + 1))
                nc.vector.tensor_tensor(oT[:, 1, pair % PAIRS, cols], G[half][:, :], oT[:, 0, pair % PAIRS, cols],
                                        ALU.subtract).then_inc(ot_ready, 1)

            def reduce_tiles(at, head, t):
                if t == 0:
                    wait(dve, mx_neg, at(HEADS, head))
                for half in range(HALVES):
                    wait(dve, max_mm, at(STEPS, HSTEPS * head + 2 * t + half + 1))
                    nc.vector.reduce_max(mx2[:, t, half:half + 1], M[half][:, :], AX.X).then_inc(reduced, 1)

            def cast_maxima(at, head):
                wait(dve, reduced, at(STEPS, HSTEPS * head + HSTEPS))
                wait(dve, mx_tr, at(HEADS, head))
                nc.vector.tensor_reduce(nmx[:, :], mx2[:, :, :], AX.X, ALU.max, negate=True).then_inc(mx_neg, 1)
                wait(dve, mx_neg, at(HEADS, head + 1))
                nc.vector.tensor_copy(mxp[:, 0:NT], nmx[:, :]).then_inc(mx_hi, 1)
                wait(dve, mx_hi, at(HEADS, head + 1))
                nc.vector.tensor_tensor(mxp[:, NT:2 * NT], nmx[:, :], mxp[:, 0:NT], ALU.subtract).then_inc(mx_cast, 1)

            def place_maxima(at, head):
                par, hd = head // 2 % 2, head % 2
                row = 0 if hd else D
                wait(dve, mx_tr, at(HEADS, head + 1))
                src = M[0][row:row + 2 * NT, 0:P // 2].bitcast(BF16).unsqueeze(1).broadcast_to([2 * NT, NT, P])
                dst = qk[row:row + 2 * NT, par, hd, Q2, :].rearrange("p (t n) -> p t n", n=P)
                nc.vector.tensor_tensor(dst, src, mask[row:row + 2 * NT, :].unsqueeze(2).broadcast_to([2 * NT, NT, P]), ALU.mult).then_inc(mx_ready, 1)

            def outputs(at, head, half):
                par, hd = head // 2 % 2, head % 2
                n = 2 * head + half
                o = O[half][:, 0:4 * (D + 1)].rearrange("p (j c) -> p j c", c=D + 1)
                wait(dve, pv_mm, at(STEPS, NT * (n + 1)))
                wait(dve, o_evac, at(2 * HEADS, n))
                nc.vector.reciprocal(rec[:, :], o[:, :, D]).then_inc(o_rec, 1)
                wait(dve, o_rec, at(2 * HEADS, n + 1))
                wait(dve, ot_mm, at(2 * PAIRS, 2 * (head // 2 - 1)))
                nc.vector.tensor_tensor(on[:, par, 4 * half:4 * half + 4, hd * D:(hd + 1) * D], o[:, :, 0:D],
                                        rec[:, :].unsqueeze(2).broadcast_to([P, 4, D]), ALU.mult).then_inc(o_evac, 1)

            def finish(at, i, ends=False):
                t, half = i // 2, i % 2
                cols = slice(half * BANK, (half + 1) * BANK)
                wait(dve, y_mm, at(2 * CT, -2 * CT + i + 1))
                if i == 0:
                    wait(dve, xh_ready, at(CT, 0))
                if t >= 2 or ends:
                    wait(dve, y_stored[t % 2], at(32, -16 if t >= 2 else -32))
                nc.vector.scalar_tensor_tensor(out=yb[:, t % 2, cols], in0=G[half][:, :],
                                               scalar=osc[:, 3 * CT + t:3 * CT + t + 1], in1=xres[:, t, cols],
                                               op0=ALU.mult, op1=ALU.add).then_inc(y_evac, 1)

            def keep_residual(at, t):
                wait(dve, y_evac, at(2 * CT, 0))
                nc.vector.tensor_scalar(xres[:, t, :], xin[:, t, :], bias[:, 3 * CT + t:3 * CT + t + 1], None,
                                        ALU.add).then_inc(res_copied, 1)

            dve.wait_ge(s_row, 64)
            for i in range(WT):
                t = TILE_ORDER[i]
                row, brow = (gamma_r, beta_r) if t < 3 * CT else (vnorm_r, vbias_r)
                dve.wait_ge(s_w[i % 4], 16 * (i // 4 + 1))
                if i >= 2:
                    dve.wait_ge(s_wsc, i - 1)
                if i == 3 * CT:
                    dve.wait_ge(s_rowcp, 1)
                nc.vector.tensor_tensor(xs[:, i % 2, 0:C], w_nat[:, i % 4, :], row, ALU.mult).then_inc(s_wg, 1)
                dve.wait_ge(s_wg, 2 * i + 1)
                nc.vector.tensor_tensor_reduce(out=scrap, in0=w_nat[:, i % 4, :], in1=brow, scale=1.0, scalar=0.0,
                                               op0=ALU.mult, op1=ALU.add, accum_out=bsum[:, t:t + 1]).then_inc(s_wg, 1)
                dve.wait_ge(s_wg, 2 * i + 2)
                link(nc.vector.tensor_tensor(bias[:, t:t + 1], bsum[:, t:t + 1], bload[:, t:t + 1], ALU.add))
                dve.wait_ge(s_pow, i + 1)
                nc.vector.tensor_scalar(fsc[:, t:t + 1], rsc[:, t:t + 1], 1e15, W_UNIT, ALU.min, ALU.mult).then_inc(s_f, 1)
                dve.wait_ge(s_f, i + 1)
                link(nc.vector.reciprocal(rsc[:, t:t + 1], fsc[:, t:t + 1]))
                link(nc.vector.tensor_scalar(osc[:, t:t + 1], rsc[:, t:t + 1], 1.0 / X_UNIT, None, ALU.mult))
                if 2 * CT <= t < 3 * CT:
                    link(nc.vector.tensor_scalar(vsc[:, t - 2 * CT:t - 2 * CT + 1], rsc[:, t:t + 1],
                                                 W_UNIT, None, ALU.mult))
                if i == CT - 1:
                    dve.wait_ge(s_const, 1)
                    for j in range(2 * CT):
                        col = vsc[:, j:j + 1] if j < CT else bias[:, CT + j:CT + j + 1]
                        last = nc.vector.tensor_scalar(diag[:, j, :], ident32[:, :], col, None, ALU.mult)
                    last.then_inc(s_diag, 1)
                if i == CT:
                    dve.wait_ge(s_rows, 1)
                    nc.vector.tensor_copy(vnorm_r, M[0][:, :])
                    nc.vector.tensor_copy(vbias_r, M[1][:, :]).then_inc(s_rowcp, 1)
                dve.wait_ge(s_whi, i + 1)
                if i >= RING:
                    dve.wait_ge(s_wtr, i - RING + 1)
                nc.vector.tensor_tensor(plo[:, i % RING, :], w_scaled[:, i % 2, :], phi[:, i % RING, :],
                                        ALU.subtract).then_inc(s_wlo, 1)
                dve.wait_ge(s_wtr, i + 1)
                src = G[i % 2][:, 0:C // 2].bitcast(F16).rearrange("p (k n) -> p k n", k=CT)
                nc.vector.tensor_copy(wT[:, 1, :, t * P:(t + 1) * P], src).then_inc(s_wtev_lo, 1)
            at = counts(dve, 0)
            group_stats(at, 0)
            group_deviation(at, 0)
            group_rstd(at, 0)
            dve.wait_ge(s_wlo, WT)
            dve.wait_ge(s_wsc, WT)
            for t in range(CT):
                normalise(at, 0, t)
            for group in range(4):
                split_qk(at, 0, group)
            split_v(at, 0, 0)
            split_v(at, 0, 1)
            for t in range(NT):
                reduce_tiles(at, 0, t)
            cast_maxima(at, 0)
            place_maxima(at, 0)

            def batch(b, first=False, last=False):
                at = counts(dve, b)
                for p in range(PAIRS):
                    has_next = not (last and p == PAIRS - 1)
                    has_prev = not (first and p == 0)
                    for t in range(PSTEPS):
                        s = PSTEPS * p + t
                        head, u = s // HSTEPS, s % HSTEPS
                        more = has_next or head < HEADS - 1
                        if s % NT == 0 and (s > 0 or not first):
                            outputs(at, (s // NT - 1) // 2, (s // NT - 1) % 2)
                        if u < NT and more:
                            reduce_tiles(at, head + 1, u)
                        if u == NT and more:
                            cast_maxima(at, head + 1)
                        if u == NT + 1 and more:
                            place_maxima(at, head + 1)
                        f = t - 2
                        if 0 <= f < OT_AT and f % QK_STEPS == QK_STEPS - 1 and has_next:
                            split_qk(at, p + 1, f // QK_STEPS)
                        if OT_AT <= f < V_AT and has_prev:
                            split_ot(at, p - 1, f - OT_AT)
                        if f in (V_AT + 3, V_AT + 7) and has_next:
                            split_v(at, p + 1, (f - V_AT) // 4)
                        if Y_AT <= t - 1 < Y_AT + 2 * CT and p == 0 and not first:
                            finish(at, t - 1 - Y_AT)
                        if p == 1 and NT + 2 <= t < NT + 2 + CT:
                            keep_residual(at, t - NT - 2)
                        if not last:
                            if p == 1 and t == PSTEPS - NT:
                                group_stats(at, 1)
                            if p == 2 and t == NT + 3:
                                group_deviation(at, 1)
                            if p == 2 and t == NT + 6:
                                group_rstd(at, 1)
                            if p == 2 and t in (Y_AT + 1, Y_AT + 3, Y_AT + 5, Y_AT + 7):
                                if t == Y_AT + 1:
                                    wait(dve, v_mm, at(2 * PAIRS, 2 * PAIRS))
                                normalise(at, 1, (t - Y_AT - 1) // 2)

            batch(0, first=True)
            with dve.Fori(1, BATCH - 1) as b:
                batch(b)
            batch(BATCH - 1, last=True)
            at = counts(dve, BATCH)
            outputs(at, -1, 1)
            split_ot(at, -1, 0)
            split_ot(at, -1, 1)
            for i in range(2 * CT):
                finish(at, i, ends=True)

        @block.gpsimd
        def _(pool):
            made = [0]

            def then(ins):
                made[0] += 1
                ins.then_inc(s_made, 1)
                pool.wait_ge(s_made, made[0])

            def constant(tile, value):
                then(nc.gpsimd.memset(tile, value))

            def select(tile, op, fill, base, pattern, mult):
                then(nc.gpsimd.affine_select(out=tile, in_=tile, compare_op=op, fill=fill, base=base,
                                             pattern=pattern, channel_multiplier=mult))

            for ident in (ident32, ident16, identb):
                constant(ident[:, :], 0.0)
                select(ident[:, :], ALU.not_equal, 1.0, 0, [[-1, P]], 1)
            constant(ones32[:, :], 1.0)
            constant(gmat[:, :], 1.0 / GSIZE)
            gm = gmat[:, :].rearrange("p (g e) -> p g e", e=GSIZE)
            select(gm, ALU.is_ge, 0.0, 0, [[-GSIZE, P // GSIZE], [0, GSIZE]], 1)
            select(gm, ALU.is_ge, 0.0, GSIZE - 1, [[GSIZE, P // GSIZE], [0, GSIZE]], -1)
            constant(mask[:, :], 0.0)
            for first_row in (0, NT, D, D + NT):
                select(mask[:, :], ALU.not_equal, 1.0, -first_row, [[-1, NT]], 1)
            for par in range(2):
                for hd, rows in ((0, slice(D, P)), (1, slice(0, D))):
                    constant(qk[rows, par, hd, K2, :].bitcast(F32), 1.0)
                    constant(qk[rows, par, hd, Q2, :].bitcast(F32), 0.0)
            constant(vb[:, :, :, :, D:D + 1], 1.0)
            nc.gpsimd.memset(halfs[:, :], -0.5).then_inc(s_const, 1)
            pool.wait_ge(s_const, 1)

            def split_q(at, pair, group):
                par, cols = pair % 2, slice(group * BANK, (group + 1) * BANK)
                wait(pool, qk_split, at(4 * PAIRS, 4 * pair + group + 1))
                nc.gpsimd.tensor_tensor(qk[0:D, par, 0, Q2, cols], qk32[0:D, group, :],
                                        qk[0:D, par, 0, Q1, cols].bitcast(F32), ALU.subtract)
                nc.gpsimd.tensor_tensor(qk[D:P, par, 1, Q2, cols], qk32[D:P, group, :],
                                        qk[D:P, par, 1, Q1, cols].bitcast(F32), ALU.subtract).then_inc(q_lo, 1)

            for i in range(WT):
                t = TILE_ORDER[i]
                pool.wait_ge(s_n2, i + 1)
                nc.gpsimd.tensor_tensor(rsc[:, t:t + 1], n2[:, t:t + 1], halfs[:, 0:1], ALU.pow).then_inc(s_pow, 1)

            def power(at, n):
                wait(pool, var_read, at(1, n + 1))
                nc.gpsimd.tensor_tensor(gn[:, RS0, :], gn[:, VAR, :], halfs[:, :], ALU.pow).then_inc(powered, 1)

            at = counts(pool, 0)
            power(at, 0)
            split_q(at, 0, 0)
            split_q(at, 0, 1)
            pool.wait_ge(q_lo, 2)

            def batch(b, first=False, last=False):
                at = counts(pool, b)
                for p in range(PAIRS):
                    has_next = not (last and p == PAIRS - 1)
                    for t in range(PSTEPS):
                        s = PSTEPS * p + t
                        wait(pool, exp_done, at(STEPS, s + 1))
                        nc.gpsimd.tensor_tensor(plo[:, s % RING, :], p32[:, s % RING, :], phi[:, s % RING, :],
                                                ALU.subtract).then_inc(plo_done, 1)
                        f = t - 2
                        if p == 2 and t == NT + 6 and not last:
                            power(at, 1)
                        if has_next and f in (QK_STEPS - 1, 2 * QK_STEPS - 1):
                            wait(pool, plo_done, at(STEPS, s + 1))
                            split_q(at, p + 1, f // QK_STEPS)
                            wait(pool, q_lo, at(2 * PAIRS, 2 * (p + 1) + f // QK_STEPS + 1))

            batch(0, first=True)
            with pool.Fori(1, BATCH - 1) as b:
                batch(b)
            batch(BATCH - 1, last=True)


_INS = ["x", "L0_conv_w_qkv", "L0_conv_b_qkv", "L0_conv_w_proj", "L0_conv_b_proj", "L0_conv_gamma", "L0_conv_beta"]


def kernel(**inputs):
    import numpy as _np
    import concourse.bacc as _bacc
    from concourse import mybir as _mybir
    from concourse.bass_utils import run_bass_kernel_spmd as _run

    nc = _bacc.Bacc("TRN2", target_bir_lowering=False, num_devices=1)
    arrays, args = {}, []
    for name in _INS:
        a = _np.ascontiguousarray(inputs[name])
        arrays[f"in_{name}_dram"] = a
        args.append(nc.dram_tensor(f"in_{name}_dram", a.shape, _mybir.dt.from_np(a.dtype), kind="ExternalInput").ap())
    shape = _np.asarray(inputs["x"]).shape
    args.append(nc.dram_tensor("out_0_dram", shape, _mybir.dt.float32, kind="ExternalOutput").ap())
    groupnorm_attention(nc, *args)
    r = _run(nc, [arrays], core_ids=[0])
    return r.results[0]["out_0_dram"]
```

```python
import math
from contextlib import ExitStack

import concourse.bass as bass
from concourse import mybir

F32 = mybir.dt.float32
F32R = mybir.dt.float32r
F16 = mybir.dt.float16
BF16 = mybir.dt.bfloat16
ALU = mybir.AluOpType
ACT = mybir.ActivationFunctionType
AX = mybir.AxisListType

P = 128
BANK = 512
HEADS = 8
GROUPS = 32
EPS = 1e-6

W_UNIT = 256.0
X_UNIT = 32.0
V_UNIT = 1.0 / 256.0
P_UNIT = 16.0


def groupnorm_attention(
    nc: bass.Bass,
    x: bass.AP,
    w_qkv: bass.AP,
    b_qkv: bass.AP,
    w_proj: bass.AP,
    b_proj: bass.AP,
    gamma: bass.AP,
    beta: bass.AP,
    out: bass.AP,
):
    BATCH, C, HI, WI = x.shape
    N = HI * WI
    D = C // HEADS
    CT = C // P
    NT = N // P
    HALVES = N // BANK
    GSIZE = C // GROUPS
    PAIRS = HEADS // 2
    HSTEPS = HALVES * NT
    PSTEPS = 2 * HSTEPS
    STEPS = HEADS * HSTEPS
    WT = 4 * CT
    assert D * 2 == P and CT == PAIRS == 4 and HALVES == 2 and NT == 8

    x_d = x.rearrange("b (t p) h w -> b t p (h w)", p=P)
    out_d = out.rearrange("b (t p) h w -> b t p (h w)", p=P)
    wqkv_d = w_qkv.rearrange("(t p) c -> t p c", p=P)
    wproj_d = w_proj.rearrange("(t p) c -> t p c", p=P)

    with ExitStack() as ctx:

        def sb(name, shape, dt):
            return ctx.enter_context(nc.sbuf_tensor(name, shape, dt))

        def sem(name):
            return ctx.enter_context(nc.semaphore(name))

        xin = sb("xin", [P, CT, N], F32)
        xres = sb("xres", [P, CT, N], F32)
        xs = sb("xs", [P, 2, N], F32)
        xh = sb("xh", [P, 2, CT, N], F16)
        wT = sb("wT", [P, 2, CT, WT * P], F16)
        K1, K2, Q1, Q2 = range(4)
        qk = sb("qk", [P, 2, 2, 4, N], F32R)
        qk32 = sb("qk32", [P, 2, BANK], F32)
        VW = 2 * D + 1
        vb = sb("vb", [P, 2, NT, 2, VW], F16)
        RING = 4
        p32 = sb("p32", [P, RING, BANK], F32)
        phi = sb("phi", [P, RING, BANK], F16)
        plo = sb("plo", [P, RING, BANK], F16)
        on = sb("on", [P, 2, NT, P], F32)
        oT = sb("oT", [P, 2, CT, N], F16)
        yb = xs
        mx2 = sb("mx2", [P, NT, 2], F32)
        nmx = sb("nmx", [P, NT], F32)
        mxp = sb("mxp", [P, 2 * NT], BF16)
        rec = sb("rec", [P, 4], F32)
        bnst = sb("bnst", [P, CT, 2, 6], F32)
        mv = sb("mv", [P, CT, 2], F32)
        gn = sb("gn", [P, 10, CT], F32)
        GMEAN, DEV, SQ, VARC, VAR, RS0, RS1, RS2, RS3, RSTD = range(10)
        n2 = sb("n2", [P, WT], F32)
        bsum = sb("bsum", [P, WT], F32)
        bias = sb("bias", [P, WT], F32)
        bload = sb("bload", [P, WT], F32)
        fsc = sb("fsc", [P, WT], F32)
        rsc = sb("rsc", [P, WT], F32)
        osc = sb("osc", [P, WT], F32)
        vsc = sb("vsc", [P, CT], F32)
        ident32 = sb("ident32", [P, P], F32)
        ident16 = sb("ident16", [P, P], F16)
        identb = sb("identb", [P, P], BF16)
        ones32 = sb("ones32", [P, P], F32)
        gmat = sb("gmat", [P, P], F32)
        mask = sb("mask", [P, NT], F32)
        carrier = sb("carrier", [P, 1], F32)
        halfs = sb("halfs", [P, CT], F32)
        w_nat = xres[:, :, :].rearrange("p a (h c) -> p (a h) c", c=C)
        WN = N // C * CT
        w_gam = oT[:, :, :, :].rearrange("p a k n -> p (a k n)").bitcast(F32).rearrange("p (s c) -> p s c", c=C)
        w_scaled = p32
        gamma_r, beta_r = (xs[:, i, 0:C] for i in range(2))
        vnorm_r, vbias_r = (on[:, 1, 4 * i:4 * i + 4, :].rearrange("p a b -> p (a b)") for i in range(2))
        diag = on[:, 0, :, :]

        def bank(name):
            return ctx.enter_context(nc.psum_tensor(name, [P, BANK], F32))

        S = [bank("S0"), bank("S1")]
        M = [bank("M0"), bank("M1")]
        O = [bank("O0"), bank("O1")]
        G = [bank("G0"), bank("G1")]

        scrap, scrap2 = O[0][:, 0:C], O[1][:, 0:C]

        s_const = sem("s_const")
        s_made = sem("s_made")
        s_row = sem("s_row")
        s_w = [sem(f"s_w{i}") for i in range(WN)]
        s_wg, s_n2, s_f, s_wsc, s_whi, s_wlo, s_wtr, s_wtev_hi, s_wtev_lo = (
            sem(n) for n in ("s_wg", "s_n2", "s_f", "s_wsc", "s_whi", "s_wlo", "s_wtr", "s_wtev_hi", "s_wtev_lo"))
        s_fold = sem("s_fold")
        s_diag, s_rows, s_rowcp = sem("s_diag"), sem("s_rows"), sem("s_rowcp")
        x_loaded = [sem(f"x_loaded{i}") for i in range(CT)]
        res_copied = sem("res_copied")
        bn_done, stats_done, mean_mm, dev_done, var_mm, var_read = (
            sem(n) for n in ("bn_done", "stats_done", "mean_mm", "dev_done", "var_mm", "var_read"))
        gn_link, powered, s_pow = sem("gn_link"), sem("powered"), sem("s_pow")
        xs_done, xhi_done, xh_ready = sem("xs_done"), sem("xhi_done"), sem("xh_ready")
        qk_mm, qk_evac, qk_hi, qk_split = (
            sem(n) for n in ("qk_mm", "qk_evac", "qk_hi", "qk_split"))
        v_mm, v_hi, v_ready = sem("v_mm"), sem("v_hi"), sem("v_ready")
        max_mm, reduced, mx_neg, mx_hi, mx_cast, mx_tr, mx_ready = (
            sem(n) for n in ("max_mm", "reduced", "mx_neg", "mx_hi", "mx_cast", "mx_tr", "mx_ready"))
        scores_mm, exp_done, plo_done, pv_mm = (
            sem(n) for n in ("scores_mm", "exp_done", "plo_done", "pv_mm"))
        o_rec, o_evac = sem("o_rec"), sem("o_evac")
        ot_mm, ot_hi, ot_ready = sem("ot_mm"), sem("ot_hi"), sem("ot_ready")
        y_mm, y_evac = sem("y_mm"), sem("y_evac")
        y_stored = [sem("y_stored0"), sem("y_stored1")]

        TILE_ORDER = [*range(2 * CT, 3 * CT), *range(2 * CT), *range(3 * CT, 4 * CT)]

        def counts(eng, b):
            kept = {}

            def at(k, c):
                if isinstance(b, int):
                    return k * b + c
                if k not in kept:
                    kept[k] = eng.snap(b * k)
                return kept[k] + c
            return at

        def wait(eng, semaphore, count):
            if isinstance(count, int) and count <= 0:
                return
            eng.wait_ge(semaphore, count)

        MAX_TILES = ((0, 2, 2, 2, 0, 2, 2, 2, 0, 2, 2), (0, 1, 2, 2, 1, 2, 2, 1, 2, 2, 1))
        MAX_AT = [next(u for u, n in enumerate(m) if n) for m in MAX_TILES]
        MX_CAST_AT = [len(m) for m in MAX_TILES]
        MX_TR_AT = [len(m) + 1 for m in MAX_TILES]
        QK_STEPS = ((0, 1, 2), (4, 5, 6), (8, 9, 10), (12, 12, 13))
        OT_AT = (3, 6)
        V_STEPS = (16, 17, 18, 19, 20, 21, 22, 23, 25, 25, 26, 26, 27, 27, 28, 29)
        V_STEPS_LAST = (8, 8, 8, 9, 9, 9, 10, 10, 13, 13, 13, 14, 14, 14, 15, 15)
        Y_STEPS = (9, 11, 13, 15, 17, 19, 21, 23)
        XS_AT, X_HI_AT, X_LO_AT = (17, 18, 22, 23), (20, 21, 25, 26), (21, 22, 26, 28)

        def max_tiles_of(head, u):
            tiles = MAX_TILES[head % 2]
            first = sum(tiles[:u])
            return range(first, first + sum(tiles[u:u + 1]))

        def v_steps(pair):
            return V_STEPS_LAST if pair == PAIRS - 1 else V_STEPS

        def v_bank(pair, i):
            return G[1] if pair == PAIRS - 1 else G[i]

        block = ctx.enter_context(nc.Block())

        @block.sync
        def _(sp):
            sp.dma_start(gamma_r, gamma.rearrange("(a c) -> a c", a=1).broadcast_to([P, C])).then_inc(s_row, 16)
            sp.dma_start(beta_r, beta.rearrange("(a c) -> a c", a=1).broadcast_to([P, C])).then_inc(s_row, 16)
            sp.dma_start(bload[:, 0:3 * CT], b_qkv.rearrange("(t p) -> p t", p=P),
                         allow_slow_non_contiguous=True).then_inc(s_row, 16)
            sp.dma_start(bload[:, 3 * CT:WT], b_proj.rearrange("(t p) -> p t", p=P),
                         allow_slow_non_contiguous=True).then_inc(s_row, 16)

            def load_w(i):
                t = TILE_ORDER[i]
                if i >= WN:
                    sp.wait_ge(s_wg, 2 * (i - WN) + 2)
                src = wqkv_d[t] if t < 3 * CT else wproj_d[t - 3 * CT]
                sp.dma_start(w_nat[:, i % WN, :], src).then_inc(s_w[i % WN], 16)

            for i in range(WN):
                load_w(i)
            for t in range(CT):
                sp.dma_start(xin[:, t, :], x_d[0, t]).then_inc(x_loaded[t], 16)
            for i in range(WN, WT):
                load_w(i)

            def store(at, last_b):
                for t in range(CT):
                    wait(sp, y_evac, at(2 * CT, -2 * CT + 2 * t + 2))
                    sp.dma_start(out_d[last_b, t], yb[:, t % 2, :]).then_inc(y_stored[t % 2], 16)

            def batch(b, first=False, last=False):
                at = counts(sp, b)
                if not first:
                    store(at, b - 1)
                if not last:
                    for t in range(CT):
                        wait(sp, res_copied, at(CT, t + 1))
                        sp.dma_start(xin[:, t, :], x_d[b + 1, t]).then_inc(x_loaded[t], 16)

            batch(0, first=True)
            with sp.Fori(1, BATCH - 1) as b:
                batch(b)
            batch(BATCH - 1, last=True)
            store(counts(sp, BATCH), BATCH - 1)
            for i in range(2):
                sp.wait_ge(y_stored[i], 16 * BATCH * CT // 2)

        @block.tensor
        def _(pe):
            def mean_matmul(at, n):
                wait(pe, stats_done, at(1, n + 1))
                nc.tensor.matmul(M[1][:, 0:CT], gmat[:, :], mv[:, :, 0], start=True, stop=True).then_inc(mean_mm, 1)

            def var_matmul(at, n):
                wait(pe, dev_done, at(1, n + 1))
                nc.tensor.matmul(M[1][:, 0:CT], gmat[:, :], gn[:, VARC, :], start=True, stop=True).then_inc(var_mm, 1)

            def project_qk(at, pair, group, part, bank, parts=3):
                col = (pair % PAIRS + PAIRS * (group // 2)) * P
                half = group % 2
                todo = [(k, w, h) for k in range(CT) for w, h in ((0, 0), (0, 1), (1, 0))]
                n = len(todo) // parts
                for i in range(part * n, part * n + n):
                    k, w, h = todo[i]
                    mm = nc.tensor.matmul(bank[:, :], wT[:, w, k, col:col + P],
                                          xh[:, h, k, half * BANK:(half + 1) * BANK],
                                          start=(i == 0), stop=(i == len(todo) - 1))
                if part == parts - 1:
                    mm.then_inc(qk_mm, 1)

            def project_v(at, pair, part, bank, parts=2):
                mt = part // parts
                col = (2 * PAIRS + pair % PAIRS) * P
                dst = bank[:, (mt % 4) * P:(mt % 4 + 1) * P]
                todo = [(k, w, h) for k in range(CT) for h, w in ((0, 0), (0, 1), (1, 0))]
                n = len(todo) // parts
                for i in range(part % parts * n, part % parts * n + n):
                    k, w, h = todo[i]
                    mm = nc.tensor.matmul(dst, xh[:, h, k, mt * P:(mt + 1) * P], wT[:, w, k, col:col + P],
                                          start=(i == 0), stop=(i == len(todo) - 1))
                if part % (4 * parts) == 4 * parts - 1:
                    mm.then_inc(v_mm, 1)

            def max_tile(at, head, i):
                par, hd, t, half = head // 2 % 2, head % 2, i // HALVES, i % HALVES
                wait(pe, reduced, at(STEPS, HSTEPS * head + i - 1))
                nc.tensor.matmul(M[half][:, :], qk[:, par, hd, Q1, t * P:(t + 1) * P],
                                 qk[:, par, hd, K1, half * BANK:(half + 1) * BANK],
                                 start=True, stop=True).then_inc(max_mm, 1)

            def max_transpose(at, head):
                row = 0 if head % 2 else D
                wait(pe, mx_cast, at(HEADS, head + 1))
                dst = M[0][row:row + 2 * NT, 0:P // 2].bitcast(BF16)
                nc.tensor.transpose(dst, mxp[:, :], identb[:, :]).then_inc(mx_tr, 1)

            def scores(at, s):
                head, u = s // HSTEPS, s % HSTEPS
                par, hd, half, mt = head // 2 % 2, head % 2, u // NT, u % NT
                wait(pe, exp_done, at(STEPS, s - 1))
                if u == 0:
                    wait(pe, mx_ready, at(HEADS, head + 1))
                q, k = slice(half * BANK, (half + 1) * BANK), slice(mt * P, (mt + 1) * P)
                nc.tensor.matmul(S[s % 2][:, :], qk[:, par, hd, K1, k], qk[:, par, hd, Q1, q], start=True, stop=False)
                nc.tensor.matmul(S[s % 2][:, :], qk[:, par, hd, K2, k], qk[:, par, hd, Q2, q],
                                 start=False, stop=True).then_inc(scores_mm, 1)

            def values(at, s):
                head, u = s // HSTEPS, s % HSTEPS
                par, hd, half, mt = head // 2 % 2, head % 2, u // NT, u % NT
                if mt == 0:
                    wait(pe, o_evac, at(2 * HEADS, 2 * head + half - 1))
                wait(pe, plo_done, at(STEPS, s + 1))
                for j in range(4):
                    cols = slice(j * P, (j + 1) * P)
                    o = O[half][:, j * (D + 1):(j + 1) * (D + 1)]
                    hi = phi[:, s % RING, cols]
                    nc.tensor.matmul(o, hi, vb[:, par, mt, hd, 0:D + 1],
                                     start=(mt == 0 and j == 0), stop=False, skip_group_check=True)
                    nc.tensor.matmul(o[:, 0:D], hi, vb[:, par, mt, hd, D + 1:VW],
                                     start=False, stop=False, skip_group_check=True)
                    mm = nc.tensor.matmul(o, plo[:, s % RING, cols], vb[:, par, mt, hd, 0:D + 1],
                                          start=False, stop=(mt == NT - 1), skip_group_check=True)
                mm.then_inc(pv_mm, 1)

            def transpose_outputs(at, pair, half, bank):
                wait(pe, o_evac, at(2 * HEADS, 4 * pair + 4))
                for j in range(4):
                    mm = nc.tensor.transpose(bank[:, j * P:(j + 1) * P], on[:, pair % 2, 4 * half + j, :],
                                             ident32[:, :])
                mm.then_inc(ot_mm, 1)

            def project_out(i, bank):
                t, half = i // 2, i % 2
                col = (3 * CT + t) * P
                todo = [(k, w, h) for k in range(CT) for w, h in ((0, 0), (0, 1), (1, 0))]
                for j, (k, w, h) in enumerate(todo):
                    mm = nc.tensor.matmul(bank[:, :], wT[:, w, k, col:col + P],
                                          oT[:, h, k, half * BANK:(half + 1) * BANK],
                                          start=(j == 0), stop=(j == len(todo) - 1))
                mm.then_inc(y_mm, 1)

            def transpose_weights(g, lo_banks):
                for i in range(CT * g, CT * g + CT):
                    pe.wait_ge(s_wlo, i + 1)
                    if i >= 2:
                        pe.wait_ge(s_wtev_hi, i - 1)
                        pe.wait_ge(s_wtev_lo, i - 1)
                    for dst, src in ((S[i % 2], phi), (lo_banks[i % 2], plo)):
                        for k in range(CT):
                            mm = nc.tensor.transpose(dst[:, 0:C // 2].bitcast(F16)[:, k * P:(k + 1) * P],
                                                     src[:, i % RING, k * P:(k + 1) * P], ident16[:, :])
                    mm.then_inc(s_wtr, 1)

            at = counts(pe, 0)
            pe.wait_ge(s_const, 1)
            pe.wait_ge(s_diag, 1)
            for j in range(2 * CT):
                mm = nc.tensor.matmul(M[j // CT][:, (j % CT) * P:(j % CT + 1) * P], ones32[:, :],
                                      diag[:, j, :], start=True, stop=True)
            mm.then_inc(s_rows, 1)
            transpose_weights(0, G)
            transpose_weights(1, G)
            pe.wait_ge(s_rowcp, 1)
            mean_matmul(at, 0)
            var_matmul(at, 0)
            transpose_weights(2, G)
            pe.wait_ge(s_wtev_hi, 3 * CT)
            pe.wait_ge(s_wtev_lo, 3 * CT)
            pe.wait_ge(xh_ready, CT)
            for group in range(4):
                wait(pe, qk_evac, group - 1)
                project_qk(at, 0, group, 0, G[group % 2], parts=1)
            for mt in range(NT):
                if mt % 4 == 0:
                    pe.wait_ge(qk_evac, 3 + mt // 4)
                project_v(at, 0, mt, G[mt // 4], parts=1)
            transpose_weights(3, O)
            pe.wait_ge(qk_split, 4)
            pe.wait_ge(var_read, 1)
            for i in range(HSTEPS):
                max_tile(at, 0, i)
            max_transpose(at, 0)
            pe.wait_ge(s_wtev_hi, WT)
            pe.wait_ge(s_wtev_lo, WT)
            scores(at, 0)
            scores(at, 1)

            def batch(b, first=False, last=False):
                at = counts(pe, b)
                for p in range(PAIRS):
                    has_next = not (last and p == PAIRS - 1)
                    has_prev = not (first and p == 0)
                    for t in range(PSTEPS):
                        s = PSTEPS * p + t
                        head, u = s // HSTEPS, s % HSTEPS
                        more = has_next or head < HEADS - 1
                        if s + 2 < STEPS or not last:
                            scores(at, s + 2)
                        if u == MAX_AT[head % 2] and more:
                            if (head + 1) % 2 == 0:
                                wait(pe, qk_split, at(4 * PAIRS, 4 * (p + 1) + 4))
                            if p == 2 and t > HSTEPS and not last:
                                wait(pe, var_read, at(1, 2))
                        for i in max_tiles_of(head, u):
                            if more:
                                max_tile(at, head + 1, i)
                        if u == MX_TR_AT[head % 2] and more:
                            max_transpose(at, head + 1)
                        if t in (1, NT // 2 + 1):
                            wait(pe, v_ready, at(2 * PAIRS, 2 * p + (1 if t == 1 else 2)))
                        if s > 0 or not first:
                            values(at, s - 1)
                        for group, part in ((g, i) for g in range(4) for i in range(3) if QK_STEPS[g][i] == t):
                            if not has_next:
                                continue
                            if part == 0:
                                wait(pe, qk_evac, at(4 * PAIRS, 4 * (p + 1) + group))
                                if group == 0:
                                    wait(pe, v_ready, at(2 * PAIRS, 2 * p + 1))
                                if group == 0 and p == PAIRS - 1:
                                    wait(pe, xh_ready, at(CT, 2 * CT))
                            project_qk(at, p + 1, group, part, G[0])
                        if t in OT_AT and has_prev:
                            half = OT_AT.index(t)
                            if half == 0:
                                wait(pe, v_ready, at(2 * PAIRS, 2 * p + 2))
                            else:
                                wait(pe, ot_ready, at(2 * PAIRS, 2 * (p - 1) + 1))
                            transpose_outputs(at, p - 1, half, G[1])
                        if t in Y_STEPS and p == 0 and not first:
                            i = Y_STEPS.index(t)
                            if i == 0:
                                wait(pe, ot_ready, at(2 * PAIRS, 0))
                            else:
                                wait(pe, y_evac, at(2 * CT, -2 * CT + i))
                            project_out(i, G[1])
                        for part in range(2 * NT):
                            if not has_next or t != v_steps(p + 1)[part]:
                                continue
                            i = part // NT
                            if part % NT == 0:
                                if v_bank(p + 1, i) is G[0]:
                                    wait(pe, qk_evac, at(4 * PAIRS, 4 * (p + 1) + 4))
                                elif p == 2 and i == 1:
                                    wait(pe, v_ready, at(2 * PAIRS, 2 * (p + 1) + 1))
                                elif p == 0:
                                    wait(pe, y_evac, at(2 * CT, 0))
                                    wait(pe, v_ready, at(2 * PAIRS, 2))
                                else:
                                    wait(pe, ot_ready, at(2 * PAIRS, 2 * p))
                            project_v(at, p + 1, part, v_bank(p + 1, i))
                        if p == 2 and t == MX_TR_AT[0] and not last:
                            wait(pe, reduced, at(STEPS, HSTEPS * (head + 1) + HSTEPS))
                            mean_matmul(at, 1)
                        if p == 2 and t == MX_TR_AT[0] + 1 and not last:
                            var_matmul(at, 1)

            batch(0, first=True)
            with pe.Fori(1, BATCH - 1) as b:
                batch(b)
            batch(BATCH - 1, last=True)
            at = counts(pe, BATCH)
            values(at, -1)
            for half in range(HALVES):
                pe.wait_ge(ot_ready, 2 * PAIRS * BATCH - 2)
                transpose_outputs(at, -1, half, G[half])
            for i in range(2 * CT):
                if i < 2:
                    pe.wait_ge(ot_ready, 2 * PAIRS * BATCH)
                else:
                    pe.wait_ge(y_evac, 2 * CT * (BATCH - 1) + i - 1)
                project_out(i, G[i % 2])

        @block.scalar
        def _(act):
            def evac_qk(at, pair, group, bank):
                t = pair % PAIRS + PAIRS * (group // 2)
                n = 4 * pair + group
                wait(act, qk_mm, at(4 * PAIRS, n + 1))
                wait(act, qk_split, at(4 * PAIRS, n - 1))
                nc.scalar.activation(qk32[:, group % 2, :], bank[:, :], ACT.Identity,
                                     bias=bias[:, t:t + 1], scale=osc[:, t:t + 1]).then_inc(qk_evac, 1)

            def evac_v(at, pair, i, bank):
                wait(act, v_mm, at(2 * PAIRS, 2 * pair + i + 1))
                wait(act, pv_mm, at(STEPS, PSTEPS * (pair - 1)))
                dst = vb[:, pair % 2, 4 * i:4 * i + 4, :, 0:D]
                src = bank[:, :].rearrange("p (m h d) -> p m h d", m=4, h=2)
                nc.scalar.mul(dst, src, V_UNIT).then_inc(v_hi, 1)

            def evac_ot(at, pair, half, bank):
                wait(act, ot_mm, at(2 * PAIRS, 2 * pair + half + 1))
                if pair == 0:
                    wait(act, y_mm, at(2 * CT, 0))
                nc.scalar.copy(oT[:, 0, pair % PAIRS, half * BANK:(half + 1) * BANK], bank[:, :]).then_inc(ot_hi, 1)

            def x_hi(at, n, t):
                wait(act, xs_done, at(CT, CT * n + t + 1))
                nc.scalar.copy(xh[:, 0, t, :], xs[:, t % 2, :]).then_inc(xhi_done, 1)

            def squares(g):
                for i in range(CT * g, CT * g + CT):
                    t = TILE_ORDER[i]
                    act.wait_ge(s_wg, 2 * i + 1)
                    if i >= 1:
                        act.wait_ge(s_n2, i)
                    nc.scalar.activation(scrap2, w_gam[:, i % WN, :], ACT.Square,
                                         accum_out=n2[:, t:t + 1]).then_inc(s_n2, 1)

            def scale_weights(g):
                act.wait_ge(s_f, g + 1)
                for i in range(CT * g, CT * g + CT):
                    t = TILE_ORDER[i]
                    if i >= RING:
                        act.wait_ge(s_wlo, i - RING + 1)
                    nc.scalar.activation(w_scaled[:, i % RING, :], w_gam[:, i % WN, :], ACT.Copy,
                                         scale=fsc[:, t:t + 1]).then_inc(s_wsc, 1)
                for i in range(CT * g, CT * g + CT):
                    act.wait_ge(s_wsc, i + 1)
                    if i >= RING:
                        act.wait_ge(s_wtr, i - RING + 1)
                    nc.scalar.copy(phi[:, i % RING, :], w_scaled[:, i % RING, :]).then_inc(s_whi, 1)

            def evac_weights(g):
                for i in range(CT * g, CT * g + CT):
                    t = TILE_ORDER[i]
                    act.wait_ge(s_wtr, i + 1)
                    src = S[i % 2][:, 0:C // 2].bitcast(F16).rearrange("p (k n) -> p k n", k=CT)
                    nc.scalar.copy(wT[:, 0, :, t * P:(t + 1) * P], src).then_inc(s_wtev_hi, 1)

            at = counts(act, 0)
            squares(0)
            squares(1)
            scale_weights(0)
            evac_weights(0)
            squares(2)
            scale_weights(1)
            evac_weights(1)
            scale_weights(2)
            evac_weights(2)
            for t in range(CT):
                x_hi(at, 0, t)
            squares(3)
            evac_qk(at, 0, 0, G[0])
            evac_qk(at, 0, 1, G[1])
            scale_weights(3)
            evac_qk(at, 0, 2, G[0])
            evac_qk(at, 0, 3, G[1])
            evac_v(at, 0, 0, G[0])
            evac_v(at, 0, 1, G[1])
            evac_weights(3)

            def batch(b, first=False, last=False):
                at = counts(act, b)
                for p in range(PAIRS):
                    has_next = not (last and p == PAIRS - 1)
                    has_prev = not (first and p == 0)
                    for t in range(PSTEPS):
                        s = PSTEPS * p + t
                        wait(act, scores_mm, at(STEPS, s + 1))
                        wait(act, pv_mm, at(STEPS, s + 1 - RING))
                        for dst in (phi, p32):
                            e = nc.scalar.activation(dst[:, s % RING, :], S[s % 2][:, :], ACT.Exp,
                                                     bias=math.log(P_UNIT), scale=float(D) ** -0.5)
                        e.then_inc(exp_done, 1)
                        f = t - 2
                        for group in range(4):
                            if has_next and f == QK_STEPS[group][-1]:
                                evac_qk(at, p + 1, group, G[0])
                        if f in OT_AT and has_prev:
                            evac_ot(at, p - 1, OT_AT.index(f), G[1])
                        for i in range(2):
                            if has_next and f == v_steps(p + 1)[NT * i + NT - 1]:
                                evac_v(at, p + 1, i, v_bank(p + 1, i))
                        if p == 2 and t in X_HI_AT and not last:
                            if t == X_HI_AT[0]:
                                wait(act, v_mm, at(2 * PAIRS, 2 * PAIRS))
                            x_hi(at, 1, X_HI_AT.index(t))

            batch(0, first=True)
            with act.Fori(1, BATCH - 1) as b:
                batch(b)
            batch(BATCH - 1, last=True)
            at = counts(act, BATCH)
            evac_ot(at, -1, 0, G[0])
            evac_ot(at, -1, 1, G[1])

        @block.vector
        def _(dve):
            fold = [0]

            def link(ins):
                fold[0] += 1
                ins.then_inc(s_fold, 1)
                dve.wait_ge(s_fold, fold[0])

            LINKS = 8

            def tile_stats(at, n, t):
                wait(dve, x_loaded[t], at(16, 16 * n + 16))
                for half in range(2):
                    last = nc.vector.bn_stats(bnst[:, t, half, :], xin[:, t, half * BANK:(half + 1) * BANK])
                last.then_inc(bn_done, 1)

            def channel_stats(at, n):
                wait(dve, bn_done, at(CT, CT * n + CT))
                nc.vector.memset(carrier[:, :], 0.0)
                for t in range(CT):
                    last = nc.vector.bn_aggr(mv[:, t, :], bnst[:, t, :, :].rearrange("p a b -> p (a b)"))
                last.then_inc(stats_done, 1)

            def gn_wait(at, n, i):
                wait(dve, gn_link, at(LINKS, LINKS * n + i))

            def group_deviation(at, n):
                wait(dve, mean_mm, at(1, n + 1))
                nc.vector.tensor_copy(gn[:, GMEAN, :], M[1][:, 0:CT]).then_inc(gn_link, 1)
                gn_wait(at, n, 1)
                nc.vector.tensor_tensor(gn[:, DEV, :], mv[:, :, 0], gn[:, GMEAN, :], ALU.subtract).then_inc(gn_link, 1)
                gn_wait(at, n, 2)
                nc.vector.tensor_tensor(gn[:, SQ, :], gn[:, DEV, :], gn[:, DEV, :], ALU.mult).then_inc(gn_link, 1)
                gn_wait(at, n, 3)
                nc.vector.tensor_tensor(gn[:, VARC, :], gn[:, SQ, :], mv[:, :, 1], ALU.add).then_inc(dev_done, 1)

            def group_variance(at, n):
                wait(dve, var_mm, at(1, n + 1))
                nc.vector.tensor_scalar(gn[:, VAR, :], M[1][:, 0:CT], EPS, None, ALU.add).then_inc(var_read, 1)

            def group_rstd(at, n):
                wait(dve, var_read, at(1, n + 1))
                wait(dve, powered, at(1, n + 1))
                nc.vector.tensor_tensor(gn[:, RS1, :], gn[:, RS0, :], gn[:, RS0, :], ALU.mult).then_inc(gn_link, 1)
                gn_wait(at, n, 4)
                nc.vector.tensor_tensor(gn[:, RS2, :], gn[:, RS1, :], gn[:, VAR, :], ALU.mult).then_inc(gn_link, 1)
                gn_wait(at, n, 5)
                nc.vector.tensor_scalar(gn[:, RS3, :], gn[:, RS2, :], -0.5 * X_UNIT, 1.5 * X_UNIT,
                                        ALU.mult, ALU.add).then_inc(gn_link, 1)
                gn_wait(at, n, 6)
                nc.vector.tensor_tensor(gn[:, RSTD, :], gn[:, RS0, :], gn[:, RS3, :], ALU.mult).then_inc(gn_link, 1)
                gn_wait(at, n, 7)
                nc.vector.tensor_copy(gn[:, SQ, :], gn[:, RSTD, :]).then_inc(gn_link, 1)
                gn_wait(at, n, 8)

            def normalise(at, n, t):
                if t < 2:
                    wait(dve, y_stored[t], at(32, 32 * (n - 1)))
                wait(dve, xh_ready, at(CT, CT * n + t - 1))
                nc.vector.tensor_scalar(xs[:, t % 2, :], xin[:, t, :], gn[:, GMEAN, t:t + 1], gn[:, RSTD, t:t + 1],
                                        ALU.subtract, ALU.mult).then_inc(xs_done, 1)

            def x_lo(at, n, t):
                wait(dve, xhi_done, at(CT, CT * n + t + 1))
                nc.vector.tensor_tensor(xh[:, 1, t, :], xs[:, t % 2, :], xh[:, 0, t, :],
                                        ALU.subtract).then_inc(xh_ready, 1)

            def split_qk_hi(at, pair, group):
                par, half = pair % 2, group % 2
                cols = slice(half * BANK, (half + 1) * BANK)
                n = 4 * pair + group
                wait(dve, qk_evac, at(4 * PAIRS, n + 1))
                wait(dve, scores_mm, at(STEPS, PSTEPS * (pair - 1)))
                for hd, rows, others in ((0, slice(0, D), slice(D, P)), (1, slice(D, P), slice(0, D))):
                    src = qk32[rows, half, :]
                    nc.vector.tensor_copy(qk[rows, par, hd, Q1 if group < 2 else K1, cols], src)
                    if group < 2:
                        last = nc.vector.tensor_copy(qk[others, par, hd, Q1, cols], src)
                    else:
                        last = nc.vector.tensor_copy(qk[rows, par, hd, K2, cols], src)
                last.then_inc(qk_hi, 1)

            def split_qk_lo(at, pair, group):
                par, half = pair % 2, group % 2
                cols = slice(half * BANK, (half + 1) * BANK)
                wait(dve, qk_hi, at(4 * PAIRS, 4 * pair + group + 1))
                for hd, rows, others in ((0, slice(0, D), slice(D, P)), (1, slice(D, P), slice(0, D))):
                    hi = qk[rows, par, hd, Q1 if group < 2 else K1, cols].bitcast(F32)
                    dst = qk[rows, par, hd, Q2, cols] if group < 2 else qk[others, par, hd, K1, cols]
                    last = nc.vector.tensor_tensor(dst, qk32[rows, half, :], hi, ALU.subtract)
                last.then_inc(qk_split, 1)

            def split_v(at, pair, i, bank):
                wait(dve, v_hi, at(2 * PAIRS, 2 * pair + i + 1))
                v = vb[:, pair % 2, 4 * i:4 * i + 4, :, :].rearrange("p m h c -> p (m h) c")
                src = bank[:, :].rearrange("p (m d) -> p m d", d=D)
                nc.vector.scalar_tensor_tensor(out=v[:, :, D + 1:VW], in0=src, scalar=V_UNIT, in1=v[:, :, 0:D],
                                               op0=ALU.mult, op1=ALU.subtract).then_inc(v_ready, 1)

            def split_ot(at, pair, half, bank):
                cols = slice(half * BANK, (half + 1) * BANK)
                wait(dve, ot_hi, at(2 * PAIRS, 2 * pair + half + 1))
                nc.vector.tensor_tensor(oT[:, 1, pair % PAIRS, cols], bank[:, :], oT[:, 0, pair % PAIRS, cols],
                                        ALU.subtract).then_inc(ot_ready, 1)

            def reduce_tile(at, head, i):
                if i == 0:
                    wait(dve, mx_neg, at(HEADS, head))
                wait(dve, max_mm, at(STEPS, HSTEPS * head + i + 1))
                nc.vector.reduce_max(mx2[:, i // 2, i % 2:i % 2 + 1], M[i % 2][:, :], AX.X).then_inc(reduced, 1)

            def cast_maxima(at, head):
                wait(dve, reduced, at(STEPS, HSTEPS * head + HSTEPS))
                wait(dve, mx_tr, at(HEADS, head))
                nc.vector.tensor_reduce(nmx[:, :], mx2[:, :, :], AX.X, ALU.max, negate=True).then_inc(mx_neg, 1)
                wait(dve, mx_neg, at(HEADS, head + 1))
                nc.vector.tensor_copy(mxp[:, 0:NT], nmx[:, :]).then_inc(mx_hi, 1)
                wait(dve, mx_hi, at(HEADS, head + 1))
                nc.vector.tensor_tensor(mxp[:, NT:2 * NT], nmx[:, :], mxp[:, 0:NT], ALU.subtract).then_inc(mx_cast, 1)

            def place_maxima(at, head):
                par, hd = head // 2 % 2, head % 2
                row = 0 if hd else D
                wait(dve, mx_tr, at(HEADS, head + 1))
                src = M[0][row:row + 2 * NT, 0:P // 2].bitcast(BF16).unsqueeze(1).broadcast_to([2 * NT, NT, P])
                dst = qk[row:row + 2 * NT, par, hd, Q2, :].rearrange("p (t n) -> p t n", n=P)
                nc.vector.tensor_tensor(dst, src, mask[row:row + 2 * NT, :].unsqueeze(2).broadcast_to([2 * NT, NT, P]), ALU.mult).then_inc(mx_ready, 1)

            def outputs(at, head, half):
                par, hd = head // 2 % 2, head % 2
                n = 2 * head + half
                o = O[half][:, 0:4 * (D + 1)].rearrange("p (j c) -> p j c", c=D + 1)
                wait(dve, pv_mm, at(STEPS, NT * (n + 1)))
                wait(dve, o_evac, at(2 * HEADS, n))
                nc.vector.reciprocal(rec[:, :], o[:, :, D]).then_inc(o_rec, 1)
                wait(dve, o_rec, at(2 * HEADS, n + 1))
                wait(dve, ot_mm, at(2 * PAIRS, 2 * (head // 2 - 1)))
                nc.vector.tensor_tensor(on[:, par, 4 * half:4 * half + 4, hd * D:(hd + 1) * D], o[:, :, 0:D],
                                        rec[:, :].unsqueeze(2).broadcast_to([P, 4, D]), ALU.mult).then_inc(o_evac, 1)

            def finish(at, i, bank, ends=False):
                t, half = i // 2, i % 2
                cols = slice(half * BANK, (half + 1) * BANK)
                wait(dve, y_mm, at(2 * CT, -2 * CT + i + 1))
                if i == 0:
                    wait(dve, xh_ready, at(CT, 0))
                if t >= 2 or ends:
                    wait(dve, y_stored[t % 2], at(32, -16 if t >= 2 else -32))
                nc.vector.scalar_tensor_tensor(out=yb[:, t % 2, cols], in0=bank[:, :],
                                               scalar=osc[:, 3 * CT + t:3 * CT + t + 1], in1=xres[:, t, cols],
                                               op0=ALU.mult, op1=ALU.add).then_inc(y_evac, 1)

            def keep_residual(at, t):
                wait(dve, y_evac, at(2 * CT, 0))
                nc.vector.tensor_scalar(xres[:, t, :], xin[:, t, :], bias[:, 3 * CT + t:3 * CT + t + 1], None,
                                        ALU.add).then_inc(res_copied, 1)

            def gamma_rows(g):
                for i in range(CT * g, CT * g + CT):
                    t = TILE_ORDER[i]
                    row, brow = (gamma_r, beta_r) if t < 3 * CT else (vnorm_r, vbias_r)
                    dve.wait_ge(s_w[i % WN], 16 * (i // WN + 1))
                    if i >= WN:
                        dve.wait_ge(s_wsc, i - WN + 1)
                    nc.vector.tensor_tensor(w_gam[:, i % WN, :], w_nat[:, i % WN, :], row, ALU.mult).then_inc(s_wg, 1)
                    if i >= 1:
                        dve.wait_ge(s_wg, 2 * i)
                    nc.vector.tensor_tensor_reduce(out=scrap, in0=w_nat[:, i % WN, :], in1=brow, scale=1.0, scalar=0.0,
                                                   op0=ALU.mult, op1=ALU.add,
                                                   accum_out=bsum[:, t:t + 1]).then_inc(s_wg, 1)

            def factors(g):
                t0 = TILE_ORDER[CT * g]
                cols = slice(t0, t0 + CT)
                dve.wait_ge(s_wg, 2 * CT * (g + 1))
                link(nc.vector.tensor_tensor(bias[:, cols], bsum[:, cols], bload[:, cols], ALU.add))
                dve.wait_ge(s_pow, g + 1)
                nc.vector.tensor_scalar(fsc[:, cols], rsc[:, cols], 1e15, W_UNIT, ALU.min, ALU.mult).then_inc(s_f, 1)
                dve.wait_ge(s_f, g + 1)
                link(nc.vector.reciprocal(rsc[:, cols], fsc[:, cols]))
                link(nc.vector.tensor_scalar(osc[:, cols], rsc[:, cols], 1.0 / X_UNIT, None, ALU.mult))
                if t0 == 2 * CT:
                    link(nc.vector.tensor_scalar(vsc[:, :], rsc[:, cols], W_UNIT, None, ALU.mult))

            def weights_lo(g):
                for i in range(CT * g, CT * g + CT):
                    dve.wait_ge(s_whi, i + 1)
                    if i >= RING:
                        dve.wait_ge(s_wtr, i - RING + 1)
                    nc.vector.tensor_tensor(plo[:, i % RING, :], w_scaled[:, i % RING, :], phi[:, i % RING, :],
                                            ALU.subtract).then_inc(s_wlo, 1)

            def evac_weights(g, banks):
                for i in range(CT * g, CT * g + CT):
                    t = TILE_ORDER[i]
                    dve.wait_ge(s_wtr, i + 1)
                    src = banks[i % 2][:, 0:C // 2].bitcast(F16).rearrange("p (k n) -> p k n", k=CT)
                    nc.vector.tensor_copy(wT[:, 1, :, t * P:(t + 1) * P], src).then_inc(s_wtev_lo, 1)

            at = counts(dve, 0)
            dve.wait_ge(s_row, 64)
            gamma_rows(0)
            gamma_rows(1)
            factors(0)
            dve.wait_ge(s_const, 1)
            for j in range(2 * CT):
                col = vsc[:, j:j + 1] if j < CT else bias[:, CT + j:CT + j + 1]
                made = nc.vector.tensor_scalar(diag[:, j, :], ident32[:, :], col, None, ALU.mult)
            made.then_inc(s_diag, 1)
            weights_lo(0)
            gamma_rows(2)
            factors(1)
            evac_weights(0, G)
            dve.wait_ge(s_rows, 1)
            nc.vector.tensor_copy(vnorm_r, M[0][:, :])
            nc.vector.tensor_copy(vbias_r, M[1][:, :]).then_inc(s_rowcp, 1)
            for t in range(CT):
                tile_stats(at, 0, t)
            channel_stats(at, 0)
            weights_lo(1)
            factors(2)
            evac_weights(1, G)
            group_deviation(at, 0)
            group_variance(at, 0)
            weights_lo(2)
            group_rstd(at, 0)
            evac_weights(2, G)
            normalise(at, 0, 0)
            normalise(at, 0, 1)
            x_lo(at, 0, 0)
            normalise(at, 0, 2)
            x_lo(at, 0, 1)
            normalise(at, 0, 3)
            x_lo(at, 0, 2)
            x_lo(at, 0, 3)
            dve.wait_ge(s_rowcp, 1)
            gamma_rows(3)
            factors(3)
            for group in range(4):
                split_qk_hi(at, 0, group)
                split_qk_lo(at, 0, group)
                if group == 1:
                    weights_lo(3)
            split_v(at, 0, 0, G[0])
            split_v(at, 0, 1, G[1])
            evac_weights(3, O)
            for i in range(HSTEPS):
                reduce_tile(at, 0, i)
            cast_maxima(at, 0)
            place_maxima(at, 0)

            def batch(b, first=False, last=False):
                at = counts(dve, b)
                for p in range(PAIRS):
                    has_next = not (last and p == PAIRS - 1)
                    has_prev = not (first and p == 0)
                    for t in range(PSTEPS):
                        s = PSTEPS * p + t
                        head, u = s // HSTEPS, s % HSTEPS
                        more = has_next or head < HEADS - 1
                        if s % NT == 1 and (s > 1 or not first):
                            outputs(at, (s // NT - 1) // 2, (s // NT - 1) % 2)
                        for i in max_tiles_of(head, u):
                            if more:
                                reduce_tile(at, head + 1, i)
                        if u == MX_CAST_AT[head % 2] and more:
                            cast_maxima(at, head + 1)
                        if u == MX_TR_AT[head % 2] and more:
                            place_maxima(at, head + 1)
                        f = t - 2
                        for group in range(4):
                            if has_next and f == QK_STEPS[group][-1]:
                                split_qk_hi(at, p + 1, group)
                            if has_next and f - 1 == QK_STEPS[group][-1]:
                                split_qk_lo(at, p + 1, group)
                        if f in OT_AT and has_prev:
                            split_ot(at, p - 1, OT_AT.index(f), G[1])
                        if t - 1 in Y_STEPS and p == 0 and not first:
                            finish(at, Y_STEPS.index(t - 1), G[1])
                        for i in range(2):
                            if has_next and f == v_steps(p + 1)[NT * i + NT - 1]:
                                split_v(at, p + 1, i, v_bank(p + 1, i))
                        if p == 1 and HSTEPS - CT <= t < HSTEPS:
                            keep_residual(at, t - HSTEPS + CT)
                        if not last:
                            if p == 1 and t >= PSTEPS - CT:
                                tile_stats(at, 1, t - PSTEPS + CT)
                            if p == 2 and t == 1:
                                channel_stats(at, 1)
                            if p == 2 and t == MX_TR_AT[0]:
                                group_deviation(at, 1)
                            if p == 2 and t == MX_TR_AT[0] + 2:
                                group_variance(at, 1)
                            if p == 2 and t == MX_TR_AT[0] + 4:
                                group_rstd(at, 1)
                            if p == 2 and t in XS_AT:
                                normalise(at, 1, XS_AT.index(t))
                            if p == 2 and t in X_LO_AT:
                                x_lo(at, 1, X_LO_AT.index(t))

            batch(0, first=True)
            with dve.Fori(1, BATCH - 1) as b:
                batch(b)
            batch(BATCH - 1, last=True)
            at = counts(dve, BATCH)
            outputs(at, -1, 1)
            split_ot(at, -1, 0, G[0])
            split_ot(at, -1, 1, G[1])
            for i in range(2 * CT):
                finish(at, i, G[i % 2], ends=True)

        @block.gpsimd
        def _(pool):
            made = [0]

            def then(ins):
                made[0] += 1
                ins.then_inc(s_made, 1)
                pool.wait_ge(s_made, made[0])

            def constant(tile, value):
                then(nc.gpsimd.memset(tile, value))

            def select(tile, op, fill, base, pattern, mult):
                then(nc.gpsimd.affine_select(out=tile, in_=tile, compare_op=op, fill=fill, base=base,
                                             pattern=pattern, channel_multiplier=mult))

            for ident in (ident32, ident16, identb):
                constant(ident[:, :], 0.0)
                select(ident[:, :], ALU.not_equal, 1.0, 0, [[-1, P]], 1)
            constant(ones32[:, :], 1.0)
            constant(gmat[:, :], 1.0 / GSIZE)
            gm = gmat[:, :].rearrange("p (g e) -> p g e", e=GSIZE)
            select(gm, ALU.is_ge, 0.0, 0, [[-GSIZE, P // GSIZE], [0, GSIZE]], 1)
            select(gm, ALU.is_ge, 0.0, GSIZE - 1, [[GSIZE, P // GSIZE], [0, GSIZE]], -1)
            constant(mask[:, :], 0.0)
            for first_row in (0, NT, D, D + NT):
                select(mask[:, :], ALU.not_equal, 1.0, -first_row, [[-1, NT]], 1)
            for par in range(2):
                for hd, rows in ((0, slice(D, P)), (1, slice(0, D))):
                    constant(qk[rows, par, hd, K2, :].bitcast(F32), 1.0)
                    constant(qk[rows, par, hd, Q2, :].bitcast(F32), 0.0)
            constant(vb[:, :, :, :, D:D + 1], 1.0)
            nc.gpsimd.memset(halfs[:, :], -0.5).then_inc(s_const, 1)
            pool.wait_ge(s_const, 1)

            def weight_norms(g):
                cols = slice(TILE_ORDER[CT * g], TILE_ORDER[CT * g] + CT)
                pool.wait_ge(s_n2, CT * (g + 1))
                nc.gpsimd.tensor_tensor(rsc[:, cols], n2[:, cols], halfs[:, :], ALU.pow).then_inc(s_pow, 1)

            def power(at, n):
                wait(pool, var_read, at(1, n + 1))
                nc.gpsimd.tensor_tensor(gn[:, RS0, :], gn[:, VAR, :], halfs[:, :], ALU.pow).then_inc(powered, 1)

            at = counts(pool, 0)
            for g in range(3):
                weight_norms(g)
            power(at, 0)
            weight_norms(3)

            def batch(b, first=False, last=False):
                at = counts(pool, b)
                for p in range(PAIRS):
                    for t in range(PSTEPS):
                        s = PSTEPS * p + t
                        wait(pool, exp_done, at(STEPS, s + 1))
                        nc.gpsimd.tensor_tensor(plo[:, s % RING, :], p32[:, s % RING, :], phi[:, s % RING, :],
                                                ALU.subtract).then_inc(plo_done, 1)
                        if p == 2 and t == MX_TR_AT[0] + 2 and not last:
                            power(at, 1)

            batch(0, first=True)
            with pool.Fori(1, BATCH - 1) as b:
                batch(b)
            batch(BATCH - 1, last=True)


_INS = ["x", "L0_conv_w_qkv", "L0_conv_b_qkv", "L0_conv_w_proj", "L0_conv_b_proj", "L0_conv_gamma", "L0_conv_beta"]


def kernel(**inputs):
    import numpy as _np
    import concourse.bacc as _bacc
    from concourse import mybir as _mybir
    from concourse.bass_utils import run_bass_kernel_spmd as _run

    nc = _bacc.Bacc("TRN2", target_bir_lowering=False, num_devices=1)
    arrays, args = {}, []
    for name in _INS:
        a = _np.ascontiguousarray(inputs[name])
        arrays[f"in_{name}_dram"] = a
        args.append(nc.dram_tensor(f"in_{name}_dram", a.shape, _mybir.dt.from_np(a.dtype), kind="ExternalInput").ap())
    shape = _np.asarray(inputs["x"]).shape
    args.append(nc.dram_tensor("out_0_dram", shape, _mybir.dt.float32, kind="ExternalOutput").ap())
    groupnorm_attention(nc, *args)
    r = _run(nc, [arrays], core_ids=[0])
    return r.results[0]["out_0_dram"]
```

```python
import math
from contextlib import ExitStack

import concourse.bass as bass
from concourse import mybir

F32 = mybir.dt.float32
F32R = mybir.dt.float32r
F16 = mybir.dt.float16
BF16 = mybir.dt.bfloat16
ALU = mybir.AluOpType
ACT = mybir.ActivationFunctionType
AX = mybir.AxisListType

P = 128
BANK = 512
HEADS = 8
GROUPS = 32
EPS = 1e-6

W_UNIT = 256.0
X_UNIT = 32.0
V_UNIT = 1.0 / W_UNIT
P_UNIT = 16.0


def groupnorm_attention(
    nc: bass.Bass,
    x: bass.AP,
    w_qkv: bass.AP,
    b_qkv: bass.AP,
    w_proj: bass.AP,
    b_proj: bass.AP,
    gamma: bass.AP,
    beta: bass.AP,
    out: bass.AP,
):
    BATCH, C, HI, WI = x.shape
    N = HI * WI
    D = C // HEADS
    CT = C // P
    NT = N // P
    HALVES = N // BANK
    GSIZE = C // GROUPS
    PAIRS = HEADS // 2
    HSTEPS = HALVES * NT
    PSTEPS = 2 * HSTEPS
    STEPS = HEADS * HSTEPS
    WT = 4 * CT
    assert D * 2 == P and CT == PAIRS == 4 and HALVES == 2 and NT == 8

    x_d = x.rearrange("b (t p) h w -> b t p (h w)", p=P)
    out_d = out.rearrange("b (t p) h w -> b t p (h w)", p=P)
    wqkv_d = w_qkv.rearrange("(t p) c -> t p c", p=P)
    wproj_d = w_proj.rearrange("(t p) c -> t p c", p=P)

    with ExitStack() as ctx:

        def sb(name, shape, dt):
            return ctx.enter_context(nc.sbuf_tensor(name, shape, dt))

        def sem(name):
            return ctx.enter_context(nc.semaphore(name))

        xin = sb("xin", [P, CT, N], F32)
        xres = sb("xres", [P, CT, N], F32)
        xs = sb("xs", [P, 2, N], F32)
        xh = sb("xh", [P, 2, CT, N], F16)
        wT = sb("wT", [P, 2, CT, WT * P], F16)
        K1, K2, Q1, Q2 = range(4)
        qk = sb("qk", [P, 2, 2, 4, N], F32R)
        qk32 = sb("qk32", [P, 2, BANK], F32)
        VW = 2 * D + 1
        vb = sb("vb", [P, 2, NT, 2, VW], F16)
        RING = 4
        p32 = sb("p32", [P, RING, BANK], F32)
        phi = sb("phi", [P, RING, BANK], F16)
        plo = sb("plo", [P, RING, BANK], F16)
        on = sb("on", [P, 2, NT, P], F32)
        oT = sb("oT", [P, 2, CT, N], F16)
        yb = xs
        mx2 = sb("mx2", [P, NT, 2], F32)
        nmx = sb("nmx", [P, NT], F32)
        mxp = sb("mxp", [P, 2 * NT], BF16)
        rec = sb("rec", [P, 4], F32)
        bnst = sb("bnst", [P, CT, 2, 6], F32)
        mv = sb("mv", [P, CT, 2], F32)
        gn = sb("gn", [P, 10, CT], F32)
        GMEAN, DEV, SQ, VARC, VAR, RS0, RS1, RS2, RS3, RSTD = range(10)
        n2 = sb("n2", [P, WT], F32)
        bsum = sb("bsum", [P, WT], F32)
        bias = sb("bias", [P, WT], F32)
        bload = sb("bload", [P, WT], F32)
        fsc = sb("fsc", [P, WT], F32)
        rsc = sb("rsc", [P, WT], F32)
        osc = sb("osc", [P, WT], F32)
        vsc = sb("vsc", [P, CT], F32)
        ident32 = sb("ident32", [P, P], F32)
        ident16 = sb("ident16", [P, P], F16)
        identb = sb("identb", [P, P], BF16)
        ones32 = sb("ones32", [P, P], F32)
        gmat = sb("gmat", [P, P], F32)
        mask = sb("mask", [P, NT], F32)
        carrier = sb("carrier", [P, 1], F32)
        halfs = sb("halfs", [P, CT], F32)
        w_nat = xres[:, :, :].rearrange("p a (h c) -> p (a h) c", c=C)
        WN = N // C * CT
        w_gam = oT[:, :, :, :].rearrange("p a k n -> p (a k n)").bitcast(F32).rearrange("p (s c) -> p s c", c=C)
        gamma_r, beta_r = (xs[:, i, 0:C] for i in range(2))
        vnorm_r, vbias_r = (on[:, 1, 4 * i:4 * i + 4, :].rearrange("p a b -> p (a b)") for i in range(2))
        diag = on[:, 0, :, :]

        def bank(name):
            return ctx.enter_context(nc.psum_tensor(name, [P, BANK], F32))

        S = [bank("S0"), bank("S1")]
        M = [bank("M0"), bank("M1")]
        O = [bank("O0"), bank("O1")]
        G = [bank("G0"), bank("G1")]

        scrap, scrap2 = O[0][:, 0:C], O[1][:, 0:C]

        s_const = sem("s_const")
        s_made = sem("s_made")
        s_filled = sem("s_filled")
        s_row = sem("s_row")
        s_w = [sem(f"s_w{i}") for i in range(WN)]
        s_wg, s_wb, s_n2, s_f, s_whi, s_wlo, s_wtr, s_wtev_hi, s_wtev_lo = (
            sem(n) for n in ("s_wg", "s_wb", "s_n2", "s_f", "s_whi", "s_wlo", "s_wtr", "s_wtev_hi", "s_wtev_lo"))
        s_fold = sem("s_fold")
        s_diag, s_rows, s_rowcp = sem("s_diag"), sem("s_rows"), sem("s_rowcp")
        x_loaded = [sem(f"x_loaded{i}") for i in range(CT)]
        res_copied = sem("res_copied")
        bn_done, stats_done, mean_mm, dev_done, var_mm, var_read = (
            sem(n) for n in ("bn_done", "stats_done", "mean_mm", "dev_done", "var_mm", "var_read"))
        gn_link, powered, s_pow = sem("gn_link"), sem("powered"), sem("s_pow")
        xs_done, xhi_done, xh_ready = sem("xs_done"), sem("xhi_done"), sem("xh_ready")
        qk_mm, qk_evac, qk_hi, qk_split = (
            sem(n) for n in ("qk_mm", "qk_evac", "qk_hi", "qk_split"))
        v_mm, v_hi, v_ready = sem("v_mm"), sem("v_hi"), sem("v_ready")
        max_mm, reduced, mx_neg, mx_hi, mx_cast, mx_tr, mx_ready = (
            sem(n) for n in ("max_mm", "reduced", "mx_neg", "mx_hi", "mx_cast", "mx_tr", "mx_ready"))
        scores_mm, exp_done, plo_done, pv_mm = (
            sem(n) for n in ("scores_mm", "exp_done", "plo_done", "pv_mm"))
        o_rec, o_evac = sem("o_rec"), sem("o_evac")
        ot_mm, ot_hi, ot_ready = sem("ot_mm"), sem("ot_hi"), sem("ot_ready")
        y_mm, y_evac = sem("y_mm"), sem("y_evac")
        y_stored = [sem("y_stored0"), sem("y_stored1")]

        TILE_ORDER = [*range(2 * CT, 3 * CT), *range(2 * CT), *range(3 * CT, 4 * CT)]

        def counts(eng, b):
            kept = {}

            def at(k, c):
                if isinstance(b, int):
                    return k * b + c
                if k not in kept:
                    kept[k] = eng.snap(b * k)
                return kept[k] + c
            return at

        def wait(eng, semaphore, count):
            if isinstance(count, int) and count <= 0:
                return
            eng.wait_ge(semaphore, count)

        MAX_TILES = ((1, 1, 2, 2, 1, 2, 2, 2, 0, 2, 1),
                     (0, 0, 0, 1, 2, 2, 2, 2, 2, 1, 1, 2, 1),
                     (0, 2, 1, 1, 2, 1, 1, 2, 1, 1, 1, 2, 1))
        MAX_FROM = HSTEPS - 2
        MX_CAST_AT = 11
        MX_TR_AT = 12
        QK_STEPS = ((0, 1, 2), (4, 5, 5), (7, 8, 9), (11, 12, 12))
        OT_AT = (3, 6)
        V_STEPS = (16, 17, 18, 19, 20, 21, 22, 22, 25, 25, 26, 26, 27, 27, 28, 29)
        V_STEPS_LAST = (9, 9, 9, 9, 10, 10, 10, 10, 13, 13, 13, 14, 14, 15, 16, 16)
        Y_STEPS = (9, 11, 14, 15, 17, 19, 21, 23)
        XS_AT, X_HI_AT, X_LO_AT = ((17, 18, 25, 29), (20, 21, 28, 32), (22, 23, 30, 33))

        def max_tiles_at(p, t):
            head, u, tiles = ((2 * p + 1, t, MAX_TILES[0]) if t < MAX_FROM
                              else (2 * p + 2, t - MAX_FROM, MAX_TILES[2 if p == 2 else 1]))
            first = sum(tiles[:u])
            return [(head, i) for i in range(first, first + sum(tiles[u:u + 1]))]

        def v_steps(pair):
            return V_STEPS_LAST if pair == PAIRS - 1 else V_STEPS

        def v_bank(pair, i):
            return G[1] if pair == PAIRS - 1 else G[i]

        block = ctx.enter_context(nc.Block())

        @block.sync
        def _(sp):
            sp.dma_start(gamma_r, gamma.rearrange("(a c) -> a c", a=1).broadcast_to([P, C])).then_inc(s_row, 16)
            sp.dma_start(beta_r, beta.rearrange("(a c) -> a c", a=1).broadcast_to([P, C])).then_inc(s_row, 16)
            sp.dma_start(bload[:, 0:3 * CT], b_qkv.rearrange("(t p) -> p t", p=P),
                         allow_slow_non_contiguous=True).then_inc(s_row, 16)
            sp.dma_start(bload[:, 3 * CT:WT], b_proj.rearrange("(t p) -> p t", p=P),
                         allow_slow_non_contiguous=True).then_inc(s_row, 16)

            def load_w(i):
                t = TILE_ORDER[i]
                if i >= WN:
                    sp.wait_ge(s_wg, i - WN + 1)
                    sp.wait_ge(s_wb, i - WN + 1)
                src = wqkv_d[t] if t < 3 * CT else wproj_d[t - 3 * CT]
                sp.dma_start(w_nat[:, i % WN, :], src).then_inc(s_w[i % WN], 16)

            for i in range(WN):
                load_w(i)
            for t in range(CT):
                sp.dma_start(xin[:, t, :], x_d[0, t]).then_inc(x_loaded[t], 16)
            for i in range(WN, WT):
                load_w(i)

            def store(at, last_b):
                for t in range(CT):
                    wait(sp, y_evac, at(2 * CT, -2 * CT + 2 * t + 2))
                    sp.dma_start(out_d[last_b, t], yb[:, t % 2, :]).then_inc(y_stored[t % 2], 16)

            def batch(b, first=False, last=False):
                at = counts(sp, b)
                if not first:
                    store(at, b - 1)
                if not last:
                    for t in range(CT):
                        wait(sp, res_copied, at(CT, t + 1))
                        sp.dma_start(xin[:, t, :], x_d[b + 1, t]).then_inc(x_loaded[t], 16)

            batch(0, first=True)
            with sp.Fori(1, BATCH - 1) as b:
                batch(b)
            batch(BATCH - 1, last=True)
            store(counts(sp, BATCH), BATCH - 1)
            for i in range(2):
                sp.wait_ge(y_stored[i], 16 * BATCH * CT // 2)

        @block.tensor
        def _(pe):
            def mean_matmul(at, n):
                wait(pe, stats_done, at(1, n + 1))
                nc.tensor.matmul(M[1][:, 0:CT], gmat[:, :], mv[:, :, 0], start=True, stop=True).then_inc(mean_mm, 1)

            def var_matmul(at, n):
                wait(pe, dev_done, at(1, n + 1))
                nc.tensor.matmul(M[1][:, 0:CT], gmat[:, :], gn[:, VARC, :], start=True, stop=True).then_inc(var_mm, 1)

            def project_qk(at, pair, group, part, bank, parts=3, first=False):
                col = (pair % PAIRS + PAIRS * (group // 2)) * P
                half = group % 2
                todo = [(k, w, h) for k in range(CT) for w, h in ((0, 0), (0, 1), (1, 0))]
                n = len(todo) // parts
                for i in range(part * n, part * n + n):
                    k, w, h = todo[i]
                    if first and i % 3 == 0:
                        wait(pe, xh_ready, k + 1)
                    mm = nc.tensor.matmul(bank[:, :], wT[:, w, k, col:col + P],
                                          xh[:, h, k, half * BANK:(half + 1) * BANK],
                                          start=(i == 0), stop=(i == len(todo) - 1))
                if part == parts - 1:
                    mm.then_inc(qk_mm, 1)

            def project_v(at, pair, part, bank, parts=2):
                mt = part // parts
                col = (2 * PAIRS + pair % PAIRS) * P
                dst = bank[:, (mt % 4) * P:(mt % 4 + 1) * P]
                todo = [(k, w, h) for k in range(CT) for h, w in ((0, 0), (0, 1), (1, 0))]
                n = len(todo) // parts
                for i in range(part % parts * n, part % parts * n + n):
                    k, w, h = todo[i]
                    mm = nc.tensor.matmul(dst, xh[:, h, k, mt * P:(mt + 1) * P], wT[:, w, k, col:col + P],
                                          start=(i == 0), stop=(i == len(todo) - 1))
                if part % (4 * parts) == 4 * parts - 1:
                    mm.then_inc(v_mm, 1)

            def max_tile(at, head, i):
                par, hd, t, half = head // 2 % 2, head % 2, i % NT, i // NT
                wait(pe, reduced, at(STEPS, HSTEPS * head + i - 1))
                nc.tensor.matmul(M[i % 2][:, :], qk[:, par, hd, Q1, t * P:(t + 1) * P],
                                 qk[:, par, hd, K1, half * BANK:(half + 1) * BANK],
                                 start=True, stop=True).then_inc(max_mm, 1)

            def max_transpose(at, head):
                row = 0 if head % 2 else D
                wait(pe, mx_cast, at(HEADS, head + 1))
                dst = M[0][row:row + 2 * NT, 0:P // 2].bitcast(BF16)
                nc.tensor.transpose(dst, mxp[:, :], identb[:, :]).then_inc(mx_tr, 1)

            def scores(at, s):
                head, u = s // HSTEPS, s % HSTEPS
                par, hd, half, mt = head // 2 % 2, head % 2, u // NT, u % NT
                wait(pe, exp_done, at(STEPS, s - 1))
                if u == 0:
                    wait(pe, mx_ready, at(HEADS, head + 1))
                q, k = slice(half * BANK, (half + 1) * BANK), slice(mt * P, (mt + 1) * P)
                nc.tensor.matmul(S[s % 2][:, :], qk[:, par, hd, K1, k], qk[:, par, hd, Q1, q], start=True, stop=False)
                nc.tensor.matmul(S[s % 2][:, :], qk[:, par, hd, K2, k], qk[:, par, hd, Q2, q],
                                 start=False, stop=True).then_inc(scores_mm, 1)

            def values(at, s):
                head, u = s // HSTEPS, s % HSTEPS
                par, hd, half, mt = head // 2 % 2, head % 2, u // NT, u % NT
                if mt == 0:
                    wait(pe, o_evac, at(2 * HEADS, 2 * head + half - 1))
                wait(pe, plo_done, at(STEPS, s + 1))
                for j in range(4):
                    cols = slice(j * P, (j + 1) * P)
                    o = O[half][:, j * (D + 1):(j + 1) * (D + 1)]
                    hi = phi[:, s % RING, cols]
                    nc.tensor.matmul(o, hi, vb[:, par, mt, hd, 0:D + 1],
                                     start=(mt == 0 and j == 0), stop=False, skip_group_check=True)
                    nc.tensor.matmul(o[:, 0:D], hi, vb[:, par, mt, hd, D + 1:VW],
                                     start=False, stop=False, skip_group_check=True)
                    mm = nc.tensor.matmul(o, plo[:, s % RING, cols], vb[:, par, mt, hd, 0:D + 1],
                                          start=False, stop=(mt == NT - 1), skip_group_check=True)
                mm.then_inc(pv_mm, 1)

            def transpose_outputs(at, pair, half, bank):
                wait(pe, o_evac, at(2 * HEADS, 4 * pair + 4))
                for j in range(4):
                    mm = nc.tensor.transpose(bank[:, j * P:(j + 1) * P], on[:, pair % 2, 4 * half + j, :],
                                             ident32[:, :])
                mm.then_inc(ot_mm, 1)

            def project_out(i, bank):
                t, half = i // 2, i % 2
                col = (3 * CT + t) * P
                todo = [(k, w, h) for k in range(CT) for w, h in ((0, 0), (0, 1), (1, 0))]
                for j, (k, w, h) in enumerate(todo):
                    mm = nc.tensor.matmul(bank[:, :], wT[:, w, k, col:col + P],
                                          oT[:, h, k, half * BANK:(half + 1) * BANK],
                                          start=(j == 0), stop=(j == len(todo) - 1))
                mm.then_inc(y_mm, 1)

            def transpose_weights(tiles, lo_banks):
                for i in tiles:
                    pe.wait_ge(s_wlo, i + 1)
                    if i >= 2:
                        pe.wait_ge(s_wtev_hi, i - 1)
                        pe.wait_ge(s_wtev_lo, i - 1)
                    for dst, src in ((S[i % 2], phi), (lo_banks[i % 2], plo)):
                        for k in range(CT):
                            mm = nc.tensor.transpose(dst[:, 0:C // 2].bitcast(F16)[:, k * P:(k + 1) * P],
                                                     src[:, i % RING, k * P:(k + 1) * P], ident16[:, :])
                    mm.then_inc(s_wtr, 1)

            at = counts(pe, 0)
            pe.wait_ge(s_const, 1)
            pe.wait_ge(s_diag, 1)
            for j in range(2 * CT):
                mm = nc.tensor.matmul(M[j // CT][:, (j % CT) * P:(j % CT + 1) * P], ones32[:, :],
                                      diag[:, j, :], start=True, stop=True)
            mm.then_inc(s_rows, 1)
            transpose_weights(range(0 * CT, 1 * CT), G)
            pe.wait_ge(s_rowcp, 1)
            mean_matmul(at, 0)
            transpose_weights(range(1 * CT, 2 * CT), G)
            var_matmul(at, 0)
            transpose_weights(range(2 * CT, 3 * CT), G)
            pe.wait_ge(s_wtev_hi, 3 * CT)
            pe.wait_ge(s_wtev_lo, 3 * CT)
            for group in range(4):
                wait(pe, qk_evac, group - 1)
                project_qk(at, 0, group, 0, G[group % 2], parts=1, first=(group == 0))
            for mt in range(NT):
                if mt % 4 == 0:
                    pe.wait_ge(qk_evac, 3 + mt // 4)
                project_v(at, 0, mt, G[mt // 4], parts=1)
            pe.wait_ge(s_filled, 1)
            pe.wait_ge(qk_split, 4)
            pe.wait_ge(var_read, 1)
            for i in range(HSTEPS):
                max_tile(at, 0, i)
                if i % 4 == 3:
                    transpose_weights([3 * CT + i // 4], O)
            max_transpose(at, 0)
            pe.wait_ge(s_wtev_hi, WT)
            pe.wait_ge(s_wtev_lo, WT)
            scores(at, 0)
            scores(at, 1)

            def batch(b, first=False, last=False):
                at = counts(pe, b)
                for p in range(PAIRS):
                    has_next = not (last and p == PAIRS - 1)
                    has_prev = not (first and p == 0)
                    for t in range(PSTEPS):
                        s = PSTEPS * p + t
                        head, u = s // HSTEPS, s % HSTEPS
                        more = has_next or head < HEADS - 1
                        if s + 2 < STEPS or not last:
                            scores(at, s + 2)
                        if u == MX_TR_AT and more:
                            max_transpose(at, head + 1)
                        if t in (1, NT // 2 + 1):
                            wait(pe, v_ready, at(2 * PAIRS, 2 * p + (1 if t == 1 else 2)))
                        if s > 0 or not first:
                            values(at, s - 1)
                        for group, part in ((g, i) for g in range(4) for i in range(3) if QK_STEPS[g][i] == t):
                            if not has_next:
                                continue
                            if part == 0:
                                wait(pe, qk_evac, at(4 * PAIRS, 4 * (p + 1) + group))
                                if group == 0:
                                    wait(pe, v_ready, at(2 * PAIRS, 2 * p + 1))
                            if group == 0 and p == PAIRS - 1:
                                wait(pe, xh_ready, at(CT, CT + part + 2))
                            project_qk(at, p + 1, group, part, G[0])
                        if t in OT_AT and has_prev:
                            half = OT_AT.index(t)
                            if half == 0:
                                wait(pe, v_ready, at(2 * PAIRS, 2 * p + 2))
                            else:
                                wait(pe, ot_ready, at(2 * PAIRS, 2 * (p - 1) + 1))
                            transpose_outputs(at, p - 1, half, G[1])
                        if t in Y_STEPS and p == 0 and not first:
                            i = Y_STEPS.index(t)
                            if i == 0:
                                wait(pe, ot_ready, at(2 * PAIRS, 0))
                            else:
                                wait(pe, y_evac, at(2 * CT, -2 * CT + i))
                            project_out(i, G[1])
                        for part in range(2 * NT):
                            if not has_next or t != v_steps(p + 1)[part]:
                                continue
                            i = part // NT
                            if part % NT == 0:
                                if v_bank(p + 1, i) is G[0]:
                                    wait(pe, qk_evac, at(4 * PAIRS, 4 * (p + 1) + 4))
                                elif p == 2 and i == 1:
                                    wait(pe, v_ready, at(2 * PAIRS, 2 * (p + 1) + 1))
                                elif p == 0:
                                    wait(pe, y_evac, at(2 * CT, 0))
                                    wait(pe, v_ready, at(2 * PAIRS, 2))
                                else:
                                    wait(pe, ot_ready, at(2 * PAIRS, 2 * p))
                            project_v(at, p + 1, part, v_bank(p + 1, i))
                        for h, i in max_tiles_at(p, t):
                            if h == HEADS and last:
                                continue
                            if h % 2 == 0 and i in (0, NT):
                                wait(pe, qk_split, at(4 * PAIRS, 4 * (p + 1) + 3 + i // NT))
                            if p == 2 and h == 6 and i == 0 and not last:
                                wait(pe, var_read, at(1, 2))
                            max_tile(at, h, i)
                        if p == 2 and t == MX_TR_AT and not last:
                            wait(pe, reduced, at(STEPS, HSTEPS * (head + 1) + HSTEPS))
                            mean_matmul(at, 1)
                        if p == 2 and t == MX_TR_AT + 1 and not last:
                            var_matmul(at, 1)

            batch(0, first=True)
            with pe.Fori(1, BATCH - 1) as b:
                batch(b)
            batch(BATCH - 1, last=True)
            at = counts(pe, BATCH)
            values(at, -1)
            for half in range(HALVES):
                pe.wait_ge(ot_ready, 2 * PAIRS * BATCH - 2)
                transpose_outputs(at, -1, half, G[half])
            for i in range(2 * CT):
                if i < 2:
                    pe.wait_ge(ot_ready, 2 * PAIRS * BATCH)
                else:
                    pe.wait_ge(y_evac, 2 * CT * (BATCH - 1) + i - 1)
                project_out(i, G[i % 2])

        @block.scalar
        def _(act):
            def evac_qk(at, pair, group, bank):
                t = pair % PAIRS + PAIRS * (group // 2)
                n = 4 * pair + group
                wait(act, qk_mm, at(4 * PAIRS, n + 1))
                wait(act, qk_split, at(4 * PAIRS, n - 1))
                nc.scalar.activation(qk32[:, group % 2, :], bank[:, :], ACT.Identity,
                                     bias=bias[:, t:t + 1], scale=osc[:, t:t + 1]).then_inc(qk_evac, 1)

            def evac_v(at, pair, i, bank):
                wait(act, v_mm, at(2 * PAIRS, 2 * pair + i + 1))
                wait(act, pv_mm, at(STEPS, PSTEPS * (pair - 1)))
                dst = vb[:, pair % 2, 4 * i:4 * i + 4, :, 0:D]
                src = bank[:, :].rearrange("p (m h d) -> p m h d", m=4, h=2)
                nc.scalar.mul(dst, src, V_UNIT).then_inc(v_hi, 1)

            def evac_ot(at, pair, half, bank):
                wait(act, ot_mm, at(2 * PAIRS, 2 * pair + half + 1))
                if pair == 0:
                    wait(act, y_mm, at(2 * CT, 0))
                nc.scalar.copy(oT[:, 0, pair % PAIRS, half * BANK:(half + 1) * BANK], bank[:, :]).then_inc(ot_hi, 1)

            def x_hi(at, n, t):
                wait(act, xs_done, at(CT, CT * n + t + 1))
                nc.scalar.copy(xh[:, 0, t, :], xs[:, t % 2, :]).then_inc(xhi_done, 1)

            def squares(g):
                for i in range(CT * g, CT * g + CT):
                    t = TILE_ORDER[i]
                    act.wait_ge(s_wg, i + 1)
                    if i >= 1:
                        act.wait_ge(s_n2, i)
                    nc.scalar.activation(scrap2, w_gam[:, i % WN, :], ACT.Square,
                                         accum_out=n2[:, t:t + 1]).then_inc(s_n2, 1)

            def weights_hi(g):
                act.wait_ge(s_f, g + 1)
                for i in range(CT * g, CT * g + CT):
                    t = TILE_ORDER[i]
                    if i >= RING:
                        act.wait_ge(s_wtr, i - RING + 1)
                    nc.scalar.activation(phi[:, i % RING, :], w_gam[:, i % WN, :], ACT.Copy,
                                         scale=fsc[:, t:t + 1]).then_inc(s_whi, 1)

            def evac_weights(g):
                for i in range(CT * g, CT * g + CT):
                    t = TILE_ORDER[i]
                    act.wait_ge(s_wtr, i + 1)
                    src = S[i % 2][:, 0:C // 2].bitcast(F16).rearrange("p (k n) -> p k n", k=CT)
                    nc.scalar.copy(wT[:, 0, :, t * P:(t + 1) * P], src).then_inc(s_wtev_hi, 1)
                    if g == 3:
                        src = O[i % 2][:, 0:C // 2].bitcast(F16).rearrange("p (k n) -> p k n", k=CT)
                        nc.scalar.copy(wT[:, 1, :, t * P:(t + 1) * P], src).then_inc(s_wtev_lo, 1)

            at = counts(act, 0)
            squares(0)
            weights_hi(0)
            squares(1)
            evac_weights(0)
            weights_hi(1)
            squares(2)
            evac_weights(1)
            weights_hi(2)
            squares(3)
            evac_weights(2)
            for t in range(CT):
                x_hi(at, 0, t)
            weights_hi(3)
            evac_qk(at, 0, 0, G[0])
            evac_qk(at, 0, 1, G[1])
            evac_qk(at, 0, 2, G[0])
            evac_qk(at, 0, 3, G[1])
            evac_v(at, 0, 0, G[0])
            evac_v(at, 0, 1, G[1])
            evac_weights(3)

            def batch(b, first=False, last=False):
                at = counts(act, b)
                for p in range(PAIRS):
                    has_next = not (last and p == PAIRS - 1)
                    has_prev = not (first and p == 0)
                    for t in range(PSTEPS):
                        s = PSTEPS * p + t
                        wait(act, scores_mm, at(STEPS, s + 1))
                        wait(act, pv_mm, at(STEPS, s + 1 - RING))
                        for dst in (phi, p32):
                            e = nc.scalar.activation(dst[:, s % RING, :], S[s % 2][:, :], ACT.Exp,
                                                     bias=math.log(P_UNIT), scale=float(D) ** -0.5)
                        e.then_inc(exp_done, 1)
                        f = t - 2
                        for group in range(4):
                            if has_next and f == QK_STEPS[group][-1]:
                                evac_qk(at, p + 1, group, G[0])
                        if f in OT_AT and has_prev:
                            evac_ot(at, p - 1, OT_AT.index(f), G[1])
                        for i in range(2):
                            if has_next and f == v_steps(p + 1)[NT * i + NT - 1]:
                                evac_v(at, p + 1, i, v_bank(p + 1, i))
                        x_t = PSTEPS * (p - 2) + t
                        if x_t in X_HI_AT and not last:
                            if x_t == X_HI_AT[0]:
                                wait(act, v_mm, at(2 * PAIRS, 2 * PAIRS))
                            x_hi(at, 1, X_HI_AT.index(x_t))

            batch(0, first=True)
            with act.Fori(1, BATCH - 1) as b:
                batch(b)
            batch(BATCH - 1, last=True)
            at = counts(act, BATCH)
            evac_ot(at, -1, 0, G[0])
            evac_ot(at, -1, 1, G[1])

        @block.vector
        def _(dve):
            fold = [0]

            def link(ins):
                fold[0] += 1
                ins.then_inc(s_fold, 1)
                dve.wait_ge(s_fold, fold[0])

            LINKS = 8

            def tile_stats(at, n, t):
                wait(dve, x_loaded[t], at(16, 16 * n + 16))
                for half in range(2):
                    last = nc.vector.bn_stats(bnst[:, t, half, :], xin[:, t, half * BANK:(half + 1) * BANK])
                last.then_inc(bn_done, 1)

            def channel_stats(at, n):
                wait(dve, bn_done, at(CT, CT * n + CT))
                nc.vector.memset(carrier[:, :], 0.0)
                for t in range(CT):
                    last = nc.vector.bn_aggr(mv[:, t, :], bnst[:, t, :, :].rearrange("p a b -> p (a b)"))
                last.then_inc(stats_done, 1)

            def gn_wait(at, n, i):
                wait(dve, gn_link, at(LINKS, LINKS * n + i))

            def group_deviation(at, n):
                wait(dve, mean_mm, at(1, n + 1))
                nc.vector.tensor_copy(gn[:, GMEAN, :], M[1][:, 0:CT]).then_inc(gn_link, 1)
                gn_wait(at, n, 1)
                nc.vector.tensor_tensor(gn[:, DEV, :], mv[:, :, 0], gn[:, GMEAN, :], ALU.subtract).then_inc(gn_link, 1)
                gn_wait(at, n, 2)
                nc.vector.tensor_tensor(gn[:, SQ, :], gn[:, DEV, :], gn[:, DEV, :], ALU.mult).then_inc(gn_link, 1)
                gn_wait(at, n, 3)
                nc.vector.tensor_tensor(gn[:, VARC, :], gn[:, SQ, :], mv[:, :, 1], ALU.add).then_inc(dev_done, 1)

            def group_variance(at, n):
                wait(dve, var_mm, at(1, n + 1))
                nc.vector.tensor_scalar(gn[:, VAR, :], M[1][:, 0:CT], EPS, None, ALU.add).then_inc(var_read, 1)

            def group_rstd(at, n):
                wait(dve, var_read, at(1, n + 1))
                wait(dve, powered, at(1, n + 1))
                nc.vector.tensor_tensor(gn[:, RS1, :], gn[:, RS0, :], gn[:, RS0, :], ALU.mult).then_inc(gn_link, 1)
                gn_wait(at, n, 4)
                nc.vector.tensor_tensor(gn[:, RS2, :], gn[:, RS1, :], gn[:, VAR, :], ALU.mult).then_inc(gn_link, 1)
                gn_wait(at, n, 5)
                nc.vector.tensor_scalar(gn[:, RS3, :], gn[:, RS2, :], -0.5 * X_UNIT, 1.5 * X_UNIT,
                                        ALU.mult, ALU.add).then_inc(gn_link, 1)
                gn_wait(at, n, 6)
                nc.vector.tensor_tensor(gn[:, RSTD, :], gn[:, RS0, :], gn[:, RS3, :], ALU.mult).then_inc(gn_link, 1)
                gn_wait(at, n, 7)
                nc.vector.tensor_copy(gn[:, SQ, :], gn[:, RSTD, :]).then_inc(gn_link, 1)
                gn_wait(at, n, 8)

            def normalise(at, n, t):
                if t < 2:
                    wait(dve, y_stored[t], at(32, 32 * (n - 1)))
                wait(dve, xh_ready, at(CT, CT * n + t - 1))
                nc.vector.tensor_scalar(xs[:, t % 2, :], xin[:, t, :], gn[:, GMEAN, t:t + 1], gn[:, RSTD, t:t + 1],
                                        ALU.subtract, ALU.mult).then_inc(xs_done, 1)

            def x_lo(at, n, t):
                wait(dve, xhi_done, at(CT, CT * n + t + 1))
                nc.vector.tensor_tensor(xh[:, 1, t, :], xs[:, t % 2, :], xh[:, 0, t, :],
                                        ALU.subtract).then_inc(xh_ready, 1)

            def split_qk_hi(at, pair, group):
                par, half = pair % 2, group % 2
                cols = slice(half * BANK, (half + 1) * BANK)
                n = 4 * pair + group
                wait(dve, qk_evac, at(4 * PAIRS, n + 1))
                wait(dve, scores_mm, at(STEPS, PSTEPS * (pair - 1)))
                for hd, rows, others in ((0, slice(0, D), slice(D, P)), (1, slice(D, P), slice(0, D))):
                    src = qk32[rows, half, :]
                    nc.vector.tensor_copy(qk[rows, par, hd, Q1 if group < 2 else K1, cols], src)
                    if group < 2:
                        last = nc.vector.tensor_copy(qk[others, par, hd, Q1, cols], src)
                    else:
                        last = nc.vector.tensor_copy(qk[rows, par, hd, K2, cols], src)
                last.then_inc(qk_hi, 1)

            def split_qk_lo(at, pair, group):
                par, half = pair % 2, group % 2
                cols = slice(half * BANK, (half + 1) * BANK)
                wait(dve, qk_hi, at(4 * PAIRS, 4 * pair + group + 1))
                for hd, rows, others in ((0, slice(0, D), slice(D, P)), (1, slice(D, P), slice(0, D))):
                    hi = qk[rows, par, hd, Q1 if group < 2 else K1, cols].bitcast(F32)
                    dst = qk[rows, par, hd, Q2, cols] if group < 2 else qk[others, par, hd, K1, cols]
                    last = nc.vector.tensor_tensor(dst, qk32[rows, half, :], hi, ALU.subtract)
                last.then_inc(qk_split, 1)

            def split_v(at, pair, i, bank):
                wait(dve, v_hi, at(2 * PAIRS, 2 * pair + i + 1))
                v = vb[:, pair % 2, 4 * i:4 * i + 4, :, :].rearrange("p m h c -> p (m h) c")
                src = bank[:, :].rearrange("p (m d) -> p m d", d=D)
                nc.vector.scalar_tensor_tensor(out=v[:, :, D + 1:VW], in0=src, scalar=V_UNIT, in1=v[:, :, 0:D],
                                               op0=ALU.mult, op1=ALU.subtract).then_inc(v_ready, 1)

            def split_ot(at, pair, half, bank):
                cols = slice(half * BANK, (half + 1) * BANK)
                wait(dve, ot_hi, at(2 * PAIRS, 2 * pair + half + 1))
                nc.vector.tensor_tensor(oT[:, 1, pair % PAIRS, cols], bank[:, :], oT[:, 0, pair % PAIRS, cols],
                                        ALU.subtract).then_inc(ot_ready, 1)

            def reduce_tile(at, head, i):
                if i == 0:
                    wait(dve, mx_neg, at(HEADS, head))
                wait(dve, max_mm, at(STEPS, HSTEPS * head + i + 1))
                nc.vector.reduce_max(mx2[:, i % NT, i // NT:i // NT + 1], M[i % 2][:, :], AX.X).then_inc(reduced, 1)

            def cast_maxima(at, head):
                wait(dve, reduced, at(STEPS, HSTEPS * head + HSTEPS))
                wait(dve, mx_tr, at(HEADS, head))
                nc.vector.tensor_reduce(nmx[:, :], mx2[:, :, :], AX.X, ALU.max, negate=True).then_inc(mx_neg, 1)
                wait(dve, mx_neg, at(HEADS, head + 1))
                nc.vector.tensor_copy(mxp[:, 0:NT], nmx[:, :]).then_inc(mx_hi, 1)
                wait(dve, mx_hi, at(HEADS, head + 1))
                nc.vector.tensor_tensor(mxp[:, NT:2 * NT], nmx[:, :], mxp[:, 0:NT], ALU.subtract).then_inc(mx_cast, 1)

            def place_maxima(at, head):
                par, hd = head // 2 % 2, head % 2
                row = 0 if hd else D
                wait(dve, mx_tr, at(HEADS, head + 1))
                src = M[0][row:row + 2 * NT, 0:P // 2].bitcast(BF16).unsqueeze(1).broadcast_to([2 * NT, NT, P])
                dst = qk[row:row + 2 * NT, par, hd, Q2, :].rearrange("p (t n) -> p t n", n=P)
                nc.vector.tensor_tensor(dst, src, mask[row:row + 2 * NT, :].unsqueeze(2).broadcast_to([2 * NT, NT, P]), ALU.mult).then_inc(mx_ready, 1)

            def outputs(at, head, half):
                par, hd = head // 2 % 2, head % 2
                n = 2 * head + half
                o = O[half][:, 0:4 * (D + 1)].rearrange("p (j c) -> p j c", c=D + 1)
                wait(dve, pv_mm, at(STEPS, NT * (n + 1)))
                wait(dve, o_evac, at(2 * HEADS, n))
                nc.vector.reciprocal(rec[:, :], o[:, :, D]).then_inc(o_rec, 1)
                wait(dve, o_rec, at(2 * HEADS, n + 1))
                wait(dve, ot_mm, at(2 * PAIRS, 2 * (head // 2 - 1)))
                nc.vector.tensor_tensor(on[:, par, 4 * half:4 * half + 4, hd * D:(hd + 1) * D], o[:, :, 0:D],
                                        rec[:, :].unsqueeze(2).broadcast_to([P, 4, D]), ALU.mult).then_inc(o_evac, 1)

            def finish(at, i, bank, ends=False):
                t, half = i // 2, i % 2
                cols = slice(half * BANK, (half + 1) * BANK)
                wait(dve, y_mm, at(2 * CT, -2 * CT + i + 1))
                if i == 0:
                    wait(dve, xh_ready, at(CT, 0))
                if t >= 2 or ends:
                    wait(dve, y_stored[t % 2], at(32, -16 if t >= 2 else -32))
                nc.vector.scalar_tensor_tensor(out=yb[:, t % 2, cols], in0=bank[:, :],
                                               scalar=osc[:, 3 * CT + t:3 * CT + t + 1], in1=xres[:, t, cols],
                                               op0=ALU.mult, op1=ALU.add).then_inc(y_evac, 1)

            def keep_residual(at, t):
                wait(dve, y_evac, at(2 * CT, 0))
                nc.vector.tensor_scalar(xres[:, t, :], xin[:, t, :], bias[:, 3 * CT + t:3 * CT + t + 1], None,
                                        ALU.add).then_inc(res_copied, 1)

            def beta_products(g):
                for i in range(CT * g, CT * g + CT):
                    t = TILE_ORDER[i]
                    dve.wait_ge(s_w[i % WN], 16 * (i // WN + 1))
                    if i >= 1:
                        dve.wait_ge(s_wb, i)
                    nc.vector.tensor_tensor_reduce(out=scrap, in0=w_nat[:, i % WN, :],
                                                   in1=beta_r if t < 3 * CT else vbias_r, scale=1.0, scalar=0.0,
                                                   op0=ALU.mult, op1=ALU.add,
                                                   accum_out=bsum[:, t:t + 1]).then_inc(s_wb, 1)

            def factors(g):
                t0 = TILE_ORDER[CT * g]
                cols = slice(t0, t0 + CT)
                dve.wait_ge(s_wb, CT * (g + 1))
                link(nc.vector.tensor_tensor(bias[:, cols], bsum[:, cols], bload[:, cols], ALU.add))
                dve.wait_ge(s_pow, g + 1)
                nc.vector.tensor_scalar(fsc[:, cols], rsc[:, cols], 1e15, W_UNIT, ALU.min, ALU.mult).then_inc(s_f, 1)
                dve.wait_ge(s_f, g + 1)
                link(nc.vector.reciprocal(rsc[:, cols], fsc[:, cols]))
                link(nc.vector.tensor_scalar(osc[:, cols], rsc[:, cols], 1.0 / X_UNIT, None, ALU.mult))
                if t0 == 2 * CT:
                    link(nc.vector.tensor_scalar(vsc[:, :], rsc[:, cols], W_UNIT, None, ALU.mult))

            def weights_lo(g):
                for i in range(CT * g, CT * g + CT):
                    t = TILE_ORDER[i]
                    dve.wait_ge(s_whi, i + 1)
                    if i >= RING:
                        dve.wait_ge(s_wtr, i - RING + 1)
                    nc.vector.scalar_tensor_tensor(out=plo[:, i % RING, :], in0=w_gam[:, i % WN, :],
                                                   scalar=fsc[:, t:t + 1], in1=phi[:, i % RING, :],
                                                   op0=ALU.mult, op1=ALU.subtract).then_inc(s_wlo, 1)

            def evac_weights(g):
                for i in range(CT * g, CT * g + CT):
                    t = TILE_ORDER[i]
                    dve.wait_ge(s_wtr, i + 1)
                    src = G[i % 2][:, 0:C // 2].bitcast(F16).rearrange("p (k n) -> p k n", k=CT)
                    nc.vector.tensor_copy(wT[:, 1, :, t * P:(t + 1) * P], src).then_inc(s_wtev_lo, 1)

            at = counts(dve, 0)
            dve.wait_ge(s_row, 64)
            beta_products(0)
            factors(0)
            dve.wait_ge(s_const, 1)
            for j in range(2 * CT):
                col = vsc[:, j:j + 1] if j < CT else bias[:, CT + j:CT + j + 1]
                made = nc.vector.tensor_scalar(diag[:, j, :], ident32[:, :], col, None, ALU.mult)
            made.then_inc(s_diag, 1)
            weights_lo(0)
            beta_products(1)
            factors(1)
            dve.wait_ge(s_rows, 1)
            nc.vector.tensor_copy(vnorm_r, M[0][:, :])
            nc.vector.tensor_copy(vbias_r, M[1][:, :]).then_inc(s_rowcp, 1)
            evac_weights(0)
            for t in range(CT):
                tile_stats(at, 0, t)
            channel_stats(at, 0)
            weights_lo(1)
            group_deviation(at, 0)
            beta_products(2)
            factors(2)
            evac_weights(1)
            group_variance(at, 0)
            group_rstd(at, 0)
            weights_lo(2)
            beta_products(3)
            factors(3)
            evac_weights(2)
            normalise(at, 0, 0)
            normalise(at, 0, 1)
            x_lo(at, 0, 0)
            normalise(at, 0, 2)
            x_lo(at, 0, 1)
            normalise(at, 0, 3)
            x_lo(at, 0, 2)
            x_lo(at, 0, 3)
            dve.wait_ge(s_filled, 1)
            for group in range(4):
                split_qk_hi(at, 0, group)
                split_qk_lo(at, 0, group)
                if group == 1:
                    weights_lo(3)
            split_v(at, 0, 0, G[0])
            split_v(at, 0, 1, G[1])
            for i in range(HSTEPS):
                reduce_tile(at, 0, i)
            cast_maxima(at, 0)
            place_maxima(at, 0)

            def batch(b, first=False, last=False):
                at = counts(dve, b)
                for p in range(PAIRS):
                    has_next = not (last and p == PAIRS - 1)
                    has_prev = not (first and p == 0)
                    for t in range(PSTEPS):
                        s = PSTEPS * p + t
                        head, u = s // HSTEPS, s % HSTEPS
                        more = has_next or head < HEADS - 1
                        if s % NT == 1 and (s > 1 or not first):
                            outputs(at, (s // NT - 1) // 2, (s // NT - 1) % 2)
                        if u == MX_CAST_AT and more:
                            cast_maxima(at, head + 1)
                        if u == MX_TR_AT and more:
                            place_maxima(at, head + 1)
                        f = t - 2
                        for group in range(4):
                            if has_next and f == QK_STEPS[group][-1]:
                                split_qk_hi(at, p + 1, group)
                            if has_next and f - 1 == QK_STEPS[group][-1]:
                                split_qk_lo(at, p + 1, group)
                        if f in OT_AT and has_prev:
                            split_ot(at, p - 1, OT_AT.index(f), G[1])
                        if t - 1 in Y_STEPS and p == 0 and not first:
                            finish(at, Y_STEPS.index(t - 1), G[1])
                        for i in range(2):
                            if has_next and f == v_steps(p + 1)[NT * i + NT - 1]:
                                split_v(at, p + 1, i, v_bank(p + 1, i))
                        if p == 1 and HSTEPS - CT <= t < HSTEPS:
                            keep_residual(at, t - HSTEPS + CT)
                        if not last:
                            if p == 1 and t >= PSTEPS - CT:
                                tile_stats(at, 1, t - PSTEPS + CT)
                            if p == 2 and t == 1:
                                channel_stats(at, 1)
                            if p == 2 and t == MX_TR_AT:
                                group_deviation(at, 1)
                            if p == 2 and t == MX_TR_AT + 2:
                                group_variance(at, 1)
                            if p == 2 and t == MX_TR_AT + 4:
                                group_rstd(at, 1)
                            x_t = PSTEPS * (p - 2) + t
                            if x_t in XS_AT:
                                normalise(at, 1, XS_AT.index(x_t))
                            if x_t in X_LO_AT:
                                x_lo(at, 1, X_LO_AT.index(x_t))
                        for h, i in max_tiles_at(p, t):
                            if h < HEADS or not last:
                                reduce_tile(at, h, i)

            batch(0, first=True)
            with dve.Fori(1, BATCH - 1) as b:
                batch(b)
            batch(BATCH - 1, last=True)
            at = counts(dve, BATCH)
            outputs(at, -1, 1)
            split_ot(at, -1, 0, G[0])
            split_ot(at, -1, 1, G[1])
            for i in range(2 * CT):
                finish(at, i, G[i % 2], ends=True)

        @block.gpsimd
        def _(pool):
            made = [0]

            def then(ins):
                made[0] += 1
                ins.then_inc(s_made, 1)
                pool.wait_ge(s_made, made[0])

            def constant(tile, value):
                then(nc.gpsimd.memset(tile, value))

            def select(tile, op, fill, base, pattern, mult):
                then(nc.gpsimd.affine_select(out=tile, in_=tile, compare_op=op, fill=fill, base=base,
                                             pattern=pattern, channel_multiplier=mult))

            constant(halfs[:, :], -0.5)
            for ident in (ident32, ident16, identb):
                constant(ident[:, :], 0.0)
                select(ident[:, :], ALU.not_equal, 1.0, 0, [[-1, P]], 1)
            constant(gmat[:, :], 1.0 / GSIZE)
            gm = gmat[:, :].rearrange("p (g e) -> p g e", e=GSIZE)
            select(gm, ALU.is_ge, 0.0, 0, [[-GSIZE, P // GSIZE], [0, GSIZE]], 1)
            select(gm, ALU.is_ge, 0.0, GSIZE - 1, [[GSIZE, P // GSIZE], [0, GSIZE]], -1)
            nc.gpsimd.memset(ones32[:, :], 1.0).then_inc(s_const, 1)

            def gamma_rows(g):
                for i in range(CT * g, CT * g + CT):
                    t = TILE_ORDER[i]
                    pool.wait_ge(s_w[i % WN], 16 * (i // WN + 1))
                    if i >= WN:
                        pool.wait_ge(s_wlo, i - WN + 1)
                    nc.gpsimd.tensor_tensor(w_gam[:, i % WN, :], w_nat[:, i % WN, :],
                                            gamma_r if t < 3 * CT else vnorm_r, ALU.mult).then_inc(s_wg, 1)

            def weight_norms(g):
                cols = slice(TILE_ORDER[CT * g], TILE_ORDER[CT * g] + CT)
                pool.wait_ge(s_n2, CT * (g + 1))
                nc.gpsimd.tensor_tensor(rsc[:, cols], n2[:, cols], halfs[:, :], ALU.pow).then_inc(s_pow, 1)

            pool.wait_ge(s_row, 64)
            for g in range(4):
                if g == 3:
                    pool.wait_ge(s_rowcp, 1)
                gamma_rows(g)
                if g < 3:
                    weight_norms(g)

            def power(at, n):
                wait(pool, var_read, at(1, n + 1))
                nc.gpsimd.tensor_tensor(gn[:, RS0, :], gn[:, VAR, :], halfs[:, :], ALU.pow).then_inc(powered, 1)

            at = counts(pool, 0)
            power(at, 0)
            weight_norms(3)
            constant(mask[:, :], 0.0)
            for first_row in (0, NT, D, D + NT):
                select(mask[:, :], ALU.not_equal, 1.0, -first_row, [[-1, NT]], 1)
            for par in range(2):
                for hd, rows in ((0, slice(D, P)), (1, slice(0, D))):
                    constant(qk[rows, par, hd, K2, :].bitcast(F32), 1.0)
                    constant(qk[rows, par, hd, Q2, :].bitcast(F32), 0.0)
            nc.gpsimd.memset(vb[:, :, :, :, D:D + 1], 1.0).then_inc(s_filled, 1)

            def batch(b, first=False, last=False):
                at = counts(pool, b)
                for p in range(PAIRS):
                    for t in range(PSTEPS):
                        s = PSTEPS * p + t
                        wait(pool, exp_done, at(STEPS, s + 1))
                        nc.gpsimd.tensor_tensor(plo[:, s % RING, :], p32[:, s % RING, :], phi[:, s % RING, :],
                                                ALU.subtract).then_inc(plo_done, 1)
                        if p == 2 and t == MX_TR_AT + 2 and not last:
                            power(at, 1)

            batch(0, first=True)
            with pool.Fori(1, BATCH - 1) as b:
                batch(b)
            batch(BATCH - 1, last=True)


_INS = ["x", "L0_conv_w_qkv", "L0_conv_b_qkv", "L0_conv_w_proj", "L0_conv_b_proj", "L0_conv_gamma", "L0_conv_beta"]


def kernel(**inputs):
    import numpy as _np
    import concourse.bacc as _bacc
    from concourse import mybir as _mybir
    from concourse.bass_utils import run_bass_kernel_spmd as _run

    nc = _bacc.Bacc("TRN2", target_bir_lowering=False, num_devices=1)
    arrays, args = {}, []
    for name in _INS:
        a = _np.ascontiguousarray(inputs[name])
        arrays[f"in_{name}_dram"] = a
        args.append(nc.dram_tensor(f"in_{name}_dram", a.shape, _mybir.dt.from_np(a.dtype), kind="ExternalInput").ap())
    shape = _np.asarray(inputs["x"]).shape
    args.append(nc.dram_tensor("out_0_dram", shape, _mybir.dt.float32, kind="ExternalOutput").ap())
    groupnorm_attention(nc, *args)
    r = _run(nc, [arrays], core_ids=[0])
    return r.results[0]["out_0_dram"]
```
